# Optimizing a Trainium2 kernel written in Bass

```python
import numpy as np
import jax
import jax.numpy as jnp

def _softmax(x, axis=-1):
    return jax.nn.softmax(x, axis=axis)

def _gelu(x):
    return jax.nn.gelu(x, approximate=True)

def _silu(x):
    return jax.nn.silu(x)

def _sigmoid(x):
    return jax.nn.sigmoid(x)

def _layernorm(x, axis=-1, eps=1e-05):
    m = jnp.mean(x, axis=axis, keepdims=True)
    v = jnp.var(x, axis=axis, keepdims=True)
    return (x - m) / jnp.sqrt(v + eps)

def _scatter_add(tgt, idx, src, axis=0):
    return tgt.at[idx].add(src)

def _segment_sum(src, seg, n):
    return jax.ops.segment_sum(src, seg, n)
kernel_name = 'mk_cond_seq_d1_seqx_r2_88543b'

def setup_inputs(seed: int=0):
    np.random.seed(seed)
    _w = jnp.asarray

    def _rec_inputs():
        import jax
        import jax.numpy as jnp
        _rk = jax.random.key(seed)
        x = -0.0002928 + 1 * jax.random.normal(jax.random.fold_in(_rk, 1), (4, 1024, 512), jnp.float32)
        _lenS = 1024 - jax.random.randint(jax.random.fold_in(_rk, 7), (4,), 0, max(1, 1024 // 4) + 1, jnp.int32)
        _lenS2 = 1024 - jax.random.randint(jax.random.fold_in(_rk, 8), (4,), 0, max(1, 1024 // 4) + 1, jnp.int32)
        cond_1024 = 0.0061147 + 1.02565 * jax.random.normal(jax.random.fold_in(_rk, 11), (4, 512), jnp.float32)
        return (x, cond_1024)
    x, cond_1024 = _rec_inputs()

    def _L0_cond_setup():
        import jax, jax.numpy as jnp
        import numpy as np
        EPS = 1e-05

        def _sln(h, w, ln_g, ln_b, Wg, bg, Wb, bb):
            mu = jnp.mean(h, axis=-1, keepdims=True)
            var = jnp.mean((h - mu) ** 2, axis=-1, keepdims=True)
            ln = (h - mu) / jnp.sqrt(var + EPS) * ln_g + ln_b
            gamma = (w @ Wg.T + bg)[:, None, :]
            beta = (w @ Wb.T + bb)[:, None, :]
            return gamma * ln + beta
        key = jax.random.key(seed)
        ks = jax.random.split(key, 20)
        B, N, D = (4, 512, 512)
        F = 4 * D
        s = lambda fan: 1.0 / np.sqrt(fan)
        inp = {'hidden': jax.random.normal(ks[0], (B, N, D), jnp.float32), 'w': jax.random.normal(ks[1], (B, D), jnp.float32), 'ln_g': jnp.ones((D,), jnp.float32), 'ln_b': jnp.zeros((D,), jnp.float32), 'Wg': jax.random.normal(ks[2], (D, D), jnp.float32) * s(D), 'bg': jnp.zeros((D,), jnp.float32), 'Wb': jax.random.normal(ks[3], (D, D), jnp.float32) * s(D), 'bb': jnp.zeros((D,), jnp.float32), 'Wqkv': jax.random.normal(ks[4], (3 * D, D), jnp.float32) * s(D), 'bqkv': jnp.zeros((3 * D,), jnp.float32), 'Wp': jax.random.normal(ks[5], (D, D), jnp.float32) * s(D), 'bp': jnp.zeros((D,), jnp.float32), 'W1': jax.random.normal(ks[6], (F, D), jnp.float32) * s(D), 'b1': jnp.zeros((F,), jnp.float32), 'W2': jax.random.normal(ks[7], (D, F), jnp.float32) * s(F), 'b2': jnp.zeros((D,), jnp.float32), 'num_heads': 16}
        return inp
    _L0_cond_all = _L0_cond_setup()
    _L0_cond_in = {k: v for k, v in _L0_cond_all.items() if k in ('ln_g', 'ln_b', 'Wg', 'bg', 'Wb', 'bb', 'Wqkv', 'bqkv', 'Wp', 'bp', 'W1', 'b1', 'W2', 'b2')}
    del _L0_cond_all
    return {'x': x, 'cond_1024': cond_1024, 'L0_cond_ln_g': _L0_cond_in['ln_g'], 'L0_cond_ln_b': _L0_cond_in['ln_b'], 'L0_cond_Wg': _L0_cond_in['Wg'], 'L0_cond_bg': _L0_cond_in['bg'], 'L0_cond_Wb': _L0_cond_in['Wb'], 'L0_cond_bb': _L0_cond_in['bb'], 'L0_cond_Wqkv': _L0_cond_in['Wqkv'], 'L0_cond_bqkv': _L0_cond_in['bqkv'], 'L0_cond_Wp': _L0_cond_in['Wp'], 'L0_cond_bp': _L0_cond_in['bp'], 'L0_cond_W1': _L0_cond_in['W1'], 'L0_cond_b1': _L0_cond_in['b1'], 'L0_cond_W2': _L0_cond_in['W2'], 'L0_cond_b2': _L0_cond_in['b2']}

def reference(x, cond_1024, L0_cond_ln_g, L0_cond_ln_b, L0_cond_Wg, L0_cond_bg, L0_cond_Wb, L0_cond_bb, L0_cond_Wqkv, L0_cond_bqkv, L0_cond_Wp, L0_cond_bp, L0_cond_W1, L0_cond_b1, L0_cond_W2, L0_cond_b2):
    import jax
    import jax.numpy as jnp

    def _L0_cond_ref(hidden, w, ln_g, ln_b, Wg, bg, Wb, bb, Wqkv, bqkv, Wp, bp, W1, b1, W2, b2, num_heads):
        import jax, jax.numpy as jnp
        import numpy as np
        EPS = 1e-05

        def _sln(h, w, ln_g, ln_b, Wg, bg, Wb, bb):
            mu = jnp.mean(h, axis=-1, keepdims=True)
            var = jnp.mean((h - mu) ** 2, axis=-1, keepdims=True)
            ln = (h - mu) / jnp.sqrt(var + EPS) * ln_g + ln_b
            gamma = (w @ Wg.T + bg)[:, None, :]
            beta = (w @ Wb.T + bb)[:, None, :]
            return gamma * ln + beta
        B, N, D = hidden.shape
        hd = D // num_heads
        h = _sln(hidden, w, ln_g, ln_b, Wg, bg, Wb, bb)
        qkv = (h @ Wqkv.T + bqkv).reshape(B, N, num_heads, hd, 3)
        q = jnp.moveaxis(qkv[..., 0], 2, 1)
        k = jnp.moveaxis(qkv[..., 1], 2, 1)
        v = jnp.moveaxis(qkv[..., 2], 2, 1)
        energy = jnp.einsum('bhqd,bhkd->bhqk', q, k)
        att = jax.nn.softmax(energy, axis=-1) / D ** 0.5
        out = jnp.einsum('bhqk,bhkd->bhqd', att, v)
        out = jnp.moveaxis(out, 1, 2).reshape(B, N, D)
        out = out @ Wp.T + bp
        h1 = out + hidden
        h2 = _sln(h1, w, ln_g, ln_b, Wg, bg, Wb, bb)
        return h2 + h1
    x = _L0_cond_ref(x, cond_1024, L0_cond_ln_g, L0_cond_ln_b, L0_cond_Wg, L0_cond_bg, L0_cond_Wb, L0_cond_bb, L0_cond_Wqkv, L0_cond_bqkv, L0_cond_Wp, L0_cond_bp, L0_cond_W1, L0_cond_b1, L0_cond_W2, L0_cond_b2, 16)
    return x

_drawn_inputs = setup_inputs


def setup_inputs(seed=0):
    import zlib

    import numpy as np

    out = dict(_drawn_inputs(seed))
    spreads = {'L0_cond_ln_g': (1.0, 0.2),
     'L0_cond_ln_b': (0.0, 0.1),
     'L0_cond_bg': (0.0, 0.1),
     'L0_cond_bb': (0.0, 0.1),
     'L0_cond_bqkv': (0.0, 0.8),
     'L0_cond_bp': (0.0, 0.1),
     'L0_cond_b1': (0.0, 0.1),
     'L0_cond_b2': (0.0, 0.1)}
    factors = {}
    for name, (base, spread) in spreads.items():
        noise = np.random.default_rng([zlib.crc32(name.encode()), seed]).standard_normal(out[name].shape)
        drawn = base * np.exp(spread * noise) if base else spread * noise
        out[name] = jnp.asarray(drawn.astype(out[name].dtype))
    for name, factor in factors.items():
        out[name] = (out[name] * factor).astype(out[name].dtype)
    return out
```

```python
from contextlib import ExitStack

import concourse.bass as bass
from concourse import mybir

ALU = mybir.AluOpType
ACT = mybir.ActivationFunctionType
AX = mybir.AxisListType
F32 = mybir.dt.float32
FR = mybir.dt.float32r
F16 = mybir.dt.float16
BF16 = mybir.dt.bfloat16

EPS = 1e-05
PROB_LIFT = 8.0

SPLIT = [(0, 0), (0, 1), (1, 0)]

LN_STEP = {0: 2, 1: 10}
TILE_STEP = {0: 6, 1: 15}
OUT_STEP = {0: 24, 1: 27}
MAX_ROW_STEP = 5


def conditioned_attention(nc, x, cond, ln_g, ln_b, Wg, bg, Wb, bb, Wqkv, bqkv, Wp, bp, out):
    B, N, D = x.shape
    HD = 32
    H = D // HD
    DC = D // 128
    NV = B * H
    NT = B * N // 128
    ITERS = NV // 4
    LEAD = N // 128 + 2
    VP = 3 * HD + 1
    NL = 2 * HD + 1
    ATT_SCALE = float(D) ** -0.5
    LAST_TILES = (NT - LEAD) // 2
    FIRST_OUTS = H // 4

    x_rows = x.rearrange("b n d -> (b n) d")
    out_rows = out.rearrange("b n d -> (b n) d")
    qk_d = nc.dram_tensor("qk_scratch", [4, B, D, N], F32, kind="Internal").ap()
    v_d = nc.dram_tensor("v_scratch", [NV, 128, N // 128, VP], BF16, kind="Internal").ap()
    att_d = nc.dram_tensor("att_scratch", [NV, N, HD], F32, kind="Internal").ap()
    gb_d = nc.dram_tensor("gain_bias_scratch", [NT // 2, 2, D], F32, kind="Internal").ap()
    att_tiles = att_d.rearrange("(b h) (t p) d -> b t p h d", b=B, p=128)
    qk_heads = qk_d.rearrange("w b (h d) n -> w (b h) d n", d=HD)
    qk_tiles = qk_d.rearrange("w b (c p) (t n) -> w b t p c n", p=128, n=128)
    v_tiles = v_d.rearrange("(b h) p t c -> b t p h c", b=B)

    with ExitStack() as ctx:
        def sb(name, shape, dt=F32):
            return ctx.enter_context(nc.sbuf_tensor(name, shape, dt))

        def sem(name):
            return ctx.enter_context(nc.semaphore(name))

        ps_st = ctx.enter_context(nc.psum_tensor("ps_st", [128, 2, 2, 512], F32))
        ps_a = ctx.enter_context(nc.psum_tensor("ps_a", [128, 2, 512], F32))
        ps_o = ctx.enter_context(nc.psum_tensor("ps_o", [128, 4, 128], F32))
        ps_w = ctx.enter_context(nc.psum_tensor("ps_w", [128, 512], F32))

        ident = sb("ident", [128, 128])
        minus_half = sb("minus_half", [128, 1])
        wqkv_s = sb("wqkv_s", [128, 2, 3, DC, 512], FR)
        wp_s = sb("wp_s", [128, 2, DC, 512], FR)
        bq_s = sb("bq_s", [128, D, 3])
        bp_s = sb("bp_s", [128, D])
        gq_s = sb("gq_s", [128, 2, D])
        go_s = sb("go_s", [128, 2, D])
        q_stack = sb("q_stack", [128, 4, N], FR)
        k_stack = sb("k_stack", [128, 4, N], FR)
        v_head = sb("v_head", [128, 4, N // 128, VP], BF16)
        p32 = sb("p32", [128, 4, 1024])
        p_hi = sb("p_hi", [128, 4, 1024], F16)
        p_lo = sb("p_lo", [128, 4, 1024], F16)
        half_max = sb("half_max", [128, 2, 16])
        neg_max = sb("neg_max", [128, 2, 8])
        max_parts = sb("max_parts", [128, 2, 16], FR)
        max_rows = sb("max_rows", [16, 2, 128], FR)
        o_sum = sb("o_sum", [128, 4, HD])
        o_rcp = sb("o_rcp", [128, 4])
        o_out = sb("o_out", [128, 2, 4, HD])
        x_tile = sb("x_tile", [128, 2, D])
        h_tile = sb("h_tile", [128, 2, D])
        bn_t = sb("bn_t", [128, 2, 6])
        mv_t = sb("mv_t", [128, 2, 2])
        st_t = sb("st_t", [128, 2, 4])
        hT_s = sb("hT_s", [128, 2, DC, 128], FR)
        rows_t = sb("rows_t", [128, 512])
        qkT_s = sb("qkT_s", [128, 4, 512], FR)
        v_rest = sb("v_rest", [128, 512])
        v_parts = sb("v_parts", [128, H, VP], BF16)
        att_t = sb("att_t", [128, 2, D])
        res_t = sb("res_t", [128, 2, D])
        oT_s = sb("oT_s", [128, 2, DC, 128], FR)
        h1_t = sb("h1_t", [128, 2, D])
        y_t = sb("y_t", [128, 2, D])
        obn_t = sb("obn_t", [128, 2, 6])
        omv_t = sb("omv_t", [128, 2, 2])
        ost_t = sb("ost_t", [128, 2, 4])
        small4 = [att_t[0:4, 0, :], att_t[0:4, 1, :], h1_t[0:4, 0, :], res_t[0:4, 0, :], res_t[0:4, 1, :]]
        condT = sb("condT", [128, DC, 4])

        s_const = sem("s_const")
        id_zero = sem("id_zero")
        s_small = sem("s_small")
        s_bias = sem("s_bias")
        raw_in = [sem(f"raw_in{r}") for r in range(4)]
        w_turned = sem("w_turned")
        w_high = sem("w_high")
        w_low = sem("w_low")
        cond_turned = sem("cond_turned")
        cond_ready = sem("cond_ready")
        mod_ready = sem("mod_ready")
        gain_chain = sem("gain_chain")
        gain_stored = sem("gain_stored")
        qk_in = [sem(f"qk_in{s}") for s in range(4)]
        v_in = [sem(f"v_in{s}") for s in range(4)]
        row_in = [sem(f"row_in{s}") for s in range(2)]
        a_ready = sem("a_ready")
        a_used = sem("a_used")
        max_chain = sem("max_chain")
        st_ready = sem("st_ready")
        exp_done = sem("exp_done")
        lo_even = sem("lo_even")
        lo_odd = sem("lo_odd")
        pv_done = sem("pv_done")
        o_chain = sem("o_chain")
        att_out = [sem(f"att_out{s}") for s in range(2)]
        x_in = [sem(f"x_in{s}") for s in range(2)]
        gq_in = sem("gq_in")
        ln_stat = sem("ln_stat")
        ln_pool = sem("ln_pool")
        tile_mm = sem("tile_mm")
        tile_hi = sem("tile_hi")
        tile_ev = sem("tile_ev")
        v_dve = sem("v_dve")
        v_pool = sem("v_pool")
        q_out = sem("q_out")
        k_out = sem("k_out")
        v_out = sem("v_out")
        att_in = [sem(f"att_in{s}") for s in range(2)]
        res_in = [sem(f"res_in{s}") for s in range(2)]
        go_in = sem("go_in")
        res_ready = sem("res_ready")
        out_mm = sem("out_mm")
        out_hi = sem("out_hi")
        out_ev = sem("out_ev")
        out_stat = sem("out_stat")
        out_pool = sem("out_pool")
        y_out = [sem(f"y_out{s}") for s in range(2)]
        ONE = 1
        start_at_one = [q_out, k_out, v_out, tile_ev, v_pool, out_mm, out_ev, out_pool]

        def need(eng, semaphore, value):
            if not isinstance(value, int) or value > 0:
                eng.wait_ge(semaphore, value)

        wqkv_rows = Wqkv.rearrange("(j c) d -> c j d", c=3)
        chunks = [("g", 0, c, Wg[c * 128:(c + 1) * 128, :]) for c in range(DC)]
        chunks += [("g", 1, c, Wb[c * 128:(c + 1) * 128, :]) for c in range(DC)]
        chunks += [("w", w, c, wqkv_rows[w, c * 128:(c + 1) * 128, :]) for w in range(3) for c in range(DC)]
        chunks += [("p", 0, c, Wp[c * 128:(c + 1) * 128, :]) for c in range(DC)]
        NG = 2 * DC
        raw = x_tile, h_tile
        raw_slot = [raw[r // 2][:, r % 2, :] for r in range(4)]
        modT = p32[:].rearrange("p a (b n) -> p (a b) n", n=512)

        A_LEAD = 16 + 8 + 1

        def lead_item(k):
            return ([(0, q) for q in range(16)] + [(1, q) for q in range(4)] + [(0, 16)]
                    + [(1, q) for q in range(4, 8)])[k]

        LEAD_SPAN = {s: (2 * s, 2 * s + 2) for s in range(9)} | {
            9: (18, 20), 10: (20, 21), 11: (21, 23), 12: (23, 25)}

        def ring_items(k):
            if k < 4:
                return [(2 * k, 1, 8 + 2 * k), (2 * k + 1, 1, 9 + 2 * k)]
            items = {4: [(8, 2, 0), (9, 2, 1)], 5: [(10, 1, 16), (11, 2, 2), (12, 2, 3)],
                     6: [(13, 2, 4), (14, 2, 5)], 7: [(15, 2, 6), (16, 2, 7)]}
            return items[k]

        def ring_uses(i, s, k, last):
            uses = []
            for pos, ahead, item in ring_items(k):
                if last and s + ahead > 3:
                    continue
                gone = 2 if last and s == 2 and item == 16 else 0
                uses.append((i + (s + ahead) // 4, (s + ahead) % 4, item,
                             A_LEAD + 17 * (4 * i + s) + pos - gone, (A_LEAD + 17 * s + pos) % 2))
            return uses

        def tile_stage(step):
            for a, first in TILE_STEP.items():
                if first <= step < first + 9:
                    return a, step - first
            return None

        def out_stage(step):
            for a, first in OUT_STEP.items():
                if first <= step < first + 3:
                    return a, step - first
            return None

        block = ctx.enter_context(nc.Block())

        @block.sync
        def _(sp):
            for r in range(4):
                sp.dma_start(raw_slot[r], chunks[r][3]).then_inc(raw_in[r], 16)
            sp.dma_start(small4[0], cond).then_inc(s_small, 16)
            for slot, row in ((1, ln_g), (2, ln_b), (3, bg), (4, bb)):
                sp.dma_start(small4[slot], row.rearrange("(a d) -> a d", a=1).to_broadcast([4, D])
                             ).then_inc(s_small, 16)
            sp.dma_start(bp_s[:], bp.rearrange("(a d) -> a d", a=1).to_broadcast([128, D])).then_inc(s_bias, 16)
            sp.dma_start(bq_s[:].rearrange("p d w -> p (d w)"),
                         bqkv.rearrange("(a d) -> a d", a=1).to_broadcast([128, 3 * D])).then_inc(s_bias, 16)
            for c in range(4, len(chunks)):
                sp.wait_ge(w_turned, c - 3)
                sp.dma_start(raw_slot[c % 4], chunks[c][3]).then_inc(raw_in[c % 4], 16)
            sp.wait_ge(gain_chain, 5)
            pairs = gb_d.rearrange("(b r) c d -> r b c d", b=B)
            for r in range(NT // 2 // B):
                sp.dma_start(pairs[r], res_t[0:4, :, :]).then_inc(gain_stored, 16)
            sp.wait_ge(gain_stored, 16 * (NT // 2 // B))
            sp.wait_ge(w_turned, len(chunks))

            def at_tile(tiles, T):
                per = N // 128
                part = tiles[bass.ds(T // per, 1), bass.ds(T % per, 1)]
                return part.rearrange("b t p c n -> (b t p) c n")

            def load_x(T, a):
                sp.dma_start(x_tile[:, a, :], x_rows[bass.ds(T * 128, 128), :]).then_inc(x_in[a], 16)

            def load_gain(dst, dst_sem, pair):
                src = gb_d[bass.ds(pair, 1), :, :].rearrange("a c d -> a (c d)")
                sp.dma_start(dst[:].rearrange("p c d -> p (c d)"),
                             src.to_broadcast([128, 2 * D])).then_inc(dst_sem, 16)

            def store_q(T):
                sp.wait_ge(tile_ev, 6 * T + 3 + ONE)
                for w in range(2):
                    sp.dma_start(at_tile(qk_tiles[w], T),
                                 qkT_s[:, w, :].bitcast(F32).rearrange("p (c n) -> p c n", n=128)).then_inc(q_out, 16)

            def store_k(T):
                sp.wait_ge(tile_ev, 6 * T + 5 + ONE)
                for w in range(2, 4):
                    sp.dma_start(at_tile(qk_tiles[w], T),
                                 qkT_s[:, w, :].bitcast(F32).rearrange("p (c n) -> p c n", n=128)).then_inc(k_out, 16)

            def store_v(T):
                sp.wait_ge(v_pool, 2 * T + 2 + ONE)
                sp.dma_start(at_tile(v_tiles, T),
                             v_parts[:]).then_inc(v_out, 16)

            def load_stacks(v, s):
                for row, part in ((0, 0), (1, 0), (2, 1)):
                    sp.dma_start(q_stack[row * HD:(row + 1) * HD, s, :].bitcast(F32),
                                 qk_heads[part, bass.ds(v, 1)].rearrange("a d n -> (a d) n")).then_inc(qk_in[s], 16)
                for row, part in ((0, 2), (1, 3), (2, 2)):
                    sp.dma_start(k_stack[row * HD:(row + 1) * HD, s, :].bitcast(F32),
                                 qk_heads[part, bass.ds(v, 1)].rearrange("a d n -> (a d) n")).then_inc(qk_in[s], 16)

            def load_v(v, s):
                sp.dma_start(v_head[:, s, :, :], v_d[bass.ds(v, 1)].rearrange("a p t c -> (a p) t c")
                             ).then_inc(v_in[s], 16)

            def store_row(v, s):
                sp.wait_ge(max_chain, 4 * v + 4)
                for part in range(2):
                    sp.dma_start(q_stack[96 + part:97 + part, s, :].bitcast(F32),
                                 max_rows[8 * part:8 * part + 8, s % 2, :].bitcast(F32)).then_inc(row_in[s % 2], 16)

            def store_att(v, half):
                sp.wait_ge(o_chain, 3 * (2 * v + half) + 3)
                sp.dma_start(att_d[bass.ds(v, 1), half * 512:(half + 1) * 512, :].rearrange(
                    "a (t p) d -> p (a t) d", p=128), o_out[:, half, :, :]).then_inc(att_out[half], 16)

            def load_outs(P0):
                for a in range(2):
                    P = P0 + a
                    sp.wait_ge(out_mm, 2 * P0 + ONE)
                    sp.wait_ge(out_pool, 5 * P0 + ONE)
                    sp.dma_start(att_t[:, a, :].rearrange("p (h d) -> p h d", h=H),
                                 at_tile(att_tiles, P)).then_inc(att_in[a], 16)
                    sp.dma_start(res_t[:, a, :], x_rows[bass.ds(P * 128, 128), :]).then_inc(res_in[a], 16)

            load_gain(gq_s, gq_in, 0)
            load_x(0, 0)
            load_x(1, 1)
            with sp.Fori(0, LEAD // 2 - 1) as p:
                sp.wait_ge(ln_pool, 8 * p + 8)
                load_gain(gq_s, gq_in, p + 1)
                for a in range(2):
                    T = 2 * p + a
                    sp.wait_ge(ln_pool, 4 * T + 4)
                    load_x(T + 2, a)
                    store_q(T)
                    store_k(T)
                    store_v(T)
            sp.wait_ge(q_out, 32 * (LEAD - 2) + ONE)
            sp.wait_ge(k_out, 32 * (LEAD - 2) + ONE)
            sp.wait_ge(v_out, 16 * (LEAD - 2) + ONE)
            for v in range(3):
                load_stacks(v, v)
                load_v(v, v)
            for a in range(2):
                T = LEAD - 2 + a
                store_q(T)
                store_k(T)
                if a == 1:
                    store_row(0, 0)
                store_v(T)

            def iteration(i, tiles, outs, first=False, last=False):
                T0 = 2 * i + LEAD
                P0 = 2 * (i - FIRST_OUTS)
                for s in range(4):
                    u = 4 * i + s
                    for k in range(8):
                        step = 8 * s + k
                        if step == 0:
                            if tiles:
                                sp.wait_ge(ln_pool, 4 * T0)
                                load_gain(gq_s, gq_in, i + LEAD // 2)
                                load_x(T0, 0)
                                load_x(T0 + 1, 1)
                            before = T0 if tiles else NT
                            sp.wait_ge(q_out, 32 * before + ONE)
                            sp.wait_ge(k_out, 32 * before + ONE)
                            sp.wait_ge(v_out, 16 * before + ONE)
                        if k == 1 and not (last and s > 0):
                            need(sp, st_ready, 8 * u)
                            load_stacks(u + 3, (s + 3) % 4)
                        if k == 3 and not (first and s == 0):
                            store_att(u - 1, 1)
                        if k == 4 and not (last and s > 0):
                            need(sp, pv_done, 8 * u)
                            load_v(u + 3, (s + 3) % 4)
                        if k == 6 and not (last and s == 3):
                            store_row(u + 1, (s + 1) % 4)
                        if k == 7:
                            store_att(u, 0)
                        if outs and step == 18:
                            load_gain(go_s, go_in, i - FIRST_OUTS)
                            load_outs(P0)
                        if tiles:
                            for a in range(2):
                                if step == TILE_STEP[a] + 5:
                                    store_q(T0 + a)
                                if step == TILE_STEP[a] + 8:
                                    store_k(T0 + a)
                                if a == 0 and step == TILE_STEP[a] + 12:
                                    store_v(T0)
                                if a == 1 and step == TILE_STEP[a] + 12:
                                    store_v(T0 + 1)

            iteration(0, True, False, first=True)
            with sp.Fori(1, FIRST_OUTS) as i:
                iteration(i, True, False)
            with sp.Fori(FIRST_OUTS, LAST_TILES) as i:
                iteration(i, True, True)
            with sp.Fori(LAST_TILES, ITERS - 1) as i:
                iteration(i, False, True)
            iteration(ITERS - 1, False, True, last=True)
            store_att(NV - 1, 1)
            for half in range(2):
                sp.wait_ge(att_out[half], 16 * NV)
            with sp.Fori(ITERS - FIRST_OUTS, ITERS) as m:
                sp.wait_ge(out_pool, 10 * m + ONE)
                load_gain(go_s, go_in, m)
                load_outs(2 * m)
            for a in range(2):
                sp.wait_ge(y_out[a], 16 * (NT // 2))

        @block.tensor
        def _(pe):
            f_ident = ident[:]

            def split_product(dst, left, right, count=range(12)):
                for n in count:
                    c, (lp, rp) = n // 3, SPLIT[n % 3]
                    mm = pe.matmul(dst, left[:, lp, c, :], right[:, rp, c, :], start=(n == 0), stop=(n == 11))
                return mm

            pe.wait_ge(s_const, 3)
            for c in range(len(chunks)):
                pe.wait_ge(raw_in[c % 4], 16 * (c // 4 + 1))
                if c >= 4:
                    if c - 4 < NG:
                        pe.wait_ge(w_high, c - 3)
                    else:
                        pe.wait_ge(w_low, c - 3 - NG)
                bank = ps_st[:, (c % 4) // 2, c % 2, :]
                for d in range(DC):
                    mm = pe.transpose(bank[:, d * 128:(d + 1) * 128], raw_slot[c % 4][:, d * 128:(d + 1) * 128], f_ident)
                mm.then_inc(w_turned, 1)
                if c == NG:
                    pe.wait_ge(s_small, 80)
                    for d in range(DC):
                        mm = pe.transpose(ps_w[:, d * 4:d * 4 + 4], small4[0][:, d * 128:(d + 1) * 128], f_ident[0:4, 0:4])
                    mm.then_inc(cond_turned, 1)
                if c == NG + 4:
                    pe.wait_ge(cond_ready, 1)
                    for m in range(2):
                        for d in range(DC):
                            mm = pe.matmul(ps_a[0:4, m, :], condT[:, d, :],
                                           modT[:, m * DC + d, :], start=(d == 0), stop=(d == DC - 1))
                    mm.then_inc(mod_ready, 1)

            def stage(T, a, k):
                if k == 0:
                    pe.wait_ge(ln_pool, 4 * T + 4)
                    pe.wait_ge(tile_ev, 6 * T + ONE)
                    for d in range(DC):
                        mm = pe.transpose(ps_w[:, d * 128:(d + 1) * 128], h_tile[:, a, d * 128:(d + 1) * 128], f_ident)
                    mm.then_inc(tile_mm, 1)
                elif k in (3, 6):
                    pe.wait_ge(tile_ev, 6 * T + (2 if k == 3 else 4) + ONE)
                    for d in range(DC):
                        mm = pe.transpose(ps_w[:, d * 128:(d + 1) * 128], rows_t[:, d * 128:(d + 1) * 128], f_ident)
                    mm.then_inc(tile_mm, 1)
                else:
                    w, part = (k - 1) // 3, (k - 1) % 3
                    if part == 0:
                        pe.wait_ge(tile_ev, 6 * T + (1, 3, 5)[w] + ONE)
                    mm = split_product(ps_w[:], hT_s[:], wqkv_s[:, :, w], range(6 * part, 6 * part + 6))
                    if part == 1:
                        mm.then_inc(tile_mm, 1)

            def out_part(pair, a, k):
                P = 2 * pair + a
                if k == 0:
                    pe.wait_ge(att_in[a], 16 * pair + 16)
                    for d in range(DC):
                        mm = pe.transpose(ps_w[:, d * 128:(d + 1) * 128], att_t[:, a, d * 128:(d + 1) * 128], f_ident)
                    mm.then_inc(out_mm, 1)
                else:
                    if k == 1:
                        pe.wait_ge(out_ev, 2 * P + 1 + ONE)
                    mm = split_product(ps_w[:], oT_s[:], wp_s[:], range(6 * (k - 1), 6 * k))
                    if k == 2:
                        mm.then_inc(out_mm, 1)

            def a_item(g, s, item, m, parity):
                v = 4 * g + s
                need(pe, a_used, m - 1)
                if item == 16:
                    pe.wait_ge(max_chain, 4 * v + 3)
                    pe.transpose(ps_a[0:16, parity, 0:128], max_parts[:, s % 2, :].bitcast(F32), f_ident).then_inc(a_ready, 1)
                    return
                t, half = item // 2, item % 2
                if item == 0:
                    pe.wait_ge(qk_in[s], 96 * g + 96)
                pe.matmul(ps_a[:, parity, :], q_stack[0:96, s, t * 128:(t + 1) * 128],
                          k_stack[0:96, s, half * 512:(half + 1) * 512], start=True, stop=True).then_inc(a_ready, 1)

            def turned_scores(g, s, k):
                if k == 0:
                    pe.wait_ge(row_in[s % 2], 64 * g + 32 * (s // 2) + 32)
                need(pe, exp_done, 32 * g + 8 * s + k - 1)
                half, pair = k // 4, k % 4
                for e in range(2):
                    t = 2 * pair + e
                    mm = pe.matmul(ps_st[:, k % 2, e, :], k_stack[0:98, s, t * 128:(t + 1) * 128],
                                   q_stack[0:98, s, half * 512:(half + 1) * 512], start=True, stop=True)
                mm.then_inc(st_ready, 1)

            def sums(g, s, k):
                half, pair = k // 4, k % 4
                v = 4 * g + s
                if k == 0:
                    pe.wait_ge(v_in[s], 16 * g + 16)
                if pair == 0:
                    need(pe, o_chain, 3 * (2 * v + half - 1) + 2)
                pe.wait_ge((lo_even, lo_odd)[k % 2], 4 * v + k // 2 + 1)
                for e in range(2):
                    for lo in range(2):
                        for t in range(4):
                            width = NL if lo else VP
                            tile = (p_lo if lo else p_hi)[:, k % 4, e * 512 + t * 128:e * 512 + (t + 1) * 128]
                            mm = pe.matmul(ps_o[:, t, 0:width], tile, v_head[:, s, 2 * pair + e, 0:width],
                                           start=(pair == 0 and e == 0 and lo == 0 and t == 0),
                                           stop=(pair == 3 and e == 1 and lo == 1 and t == 3), skip_group_check=True)
                mm.then_inc(pv_done, 1)

            with pe.Fori(0, LEAD // 2 - 1) as p:
                for a in range(2):
                    for k in range(9):
                        if k == 0 and a == 0:
                            pe.wait_ge(w_low, len(chunks) - NG)
                        stage(2 * p + a, a, k)
            for step in range(18):
                for m in range(*LEAD_SPAN.get(step, (0, 0))):
                    v, item = lead_item(m)
                    a_item(0, v, item, m, m % 2)
                stage(LEAD - 2 + step // 9, step // 9, step % 9)
            turned_scores(0, 0, 0)

            def iteration(i, tiles, outs, first=False, last=False):
                T0 = 2 * i + LEAD
                P0 = 2 * (i - FIRST_OUTS)
                for s in range(4):
                    u = 4 * i + s
                    for k in range(8):
                        step = 8 * s + k
                        for use in ring_uses(i, s, k, last):
                            a_item(*use)
                        if k < 7:
                            turned_scores(i, s, k + 1)
                        elif not (last and s == 3):
                            turned_scores(i + (s + 1) // 4, (s + 1) % 4, 0)
                        if k >= 2:
                            sums(i, s, k - 2)
                        elif not (first and s == 0):
                            sums(i - (s == 0), (s - 1) % 4, k + 6)
                        if tiles and tile_stage(step):
                            a, part = tile_stage(step)
                            stage(T0 + a, a, part)
                        if outs and out_stage(step):
                            a, part = out_stage(step)
                            if part == 0:
                                pe.wait_ge(tile_ev, (6 * (T0 + 2) if tiles else 6 * NT) + ONE)
                                pe.wait_ge(out_ev, 2 * (P0 + a) + ONE)
                            out_part(i - FIRST_OUTS, a, part)

            iteration(0, True, False, first=True)
            with pe.Fori(1, FIRST_OUTS) as i:
                iteration(i, True, False)
            with pe.Fori(FIRST_OUTS, LAST_TILES) as i:
                iteration(i, True, True)
            with pe.Fori(LAST_TILES, ITERS - 1) as i:
                iteration(i, False, True)
            iteration(ITERS - 1, False, True, last=True)
            for k in (6, 7):
                sums(ITERS - 1, 3, k)
            with pe.Fori(ITERS - FIRST_OUTS, ITERS) as m:
                for a in range(2):
                    pe.wait_ge(out_ev, 2 * (2 * m + a) + ONE)
                    for k in range(3):
                        out_part(m, a, k)

        @block.scalar
        def _(act):
            for c in range(len(chunks)):
                kind, w, part, _ = chunks[c]
                act.wait_ge(w_turned, c + 1)
                bank = ps_st[:, (c % 4) // 2, c % 2, :].rearrange("p (c n) -> p c n", c=DC)
                if kind == "g":
                    dst = modT[:, w * DC:(w + 1) * DC, part * 128:(part + 1) * 128]
                else:
                    dst = (wqkv_s[:, 0, w] if kind == "w" else wp_s[:, 0])[:, :, part * 128:(part + 1) * 128]
                nc.scalar.activation(dst, bank, ACT.Copy).then_inc(w_high, 1)
                if c == NG:
                    act.wait_ge(cond_turned, 1)
                    nc.scalar.activation(condT[:].rearrange("p c n -> p (c n)"), ps_w[:, 0:4 * DC], ACT.Copy
                                         ).then_inc(cond_ready, 1)

            def tile_high(T, k):
                act.wait_ge(tile_mm, 6 * T + 1 + 2 * k)
                if k == 0:
                    dst = hT_s[:, 0].rearrange("p c n -> p (c n)")
                else:
                    act.wait_ge((q_out, k_out)[k - 1], 32 * T + ONE)
                    dst = qkT_s[:, 2 * k - 2, :]
                nc.scalar.activation(dst, ps_w[:], ACT.Copy).then_inc(tile_hi, 1)

            def out_high(P):
                act.wait_ge(out_mm, 2 * P + 1 + ONE)
                nc.scalar.activation(oT_s[:, 0].rearrange("p c n -> p (c n)"), ps_w[:], ACT.Copy).then_inc(out_hi, 1)

            def exps(i, step):
                n, k = 32 * i + step, step % 8
                act.wait_ge(st_ready, n + 1)
                need(act, (lo_even, lo_odd)[k % 2], 16 * i + step // 2 - 1)
                scores = ps_st[:, k % 2, :, :].rearrange("p a n -> p (a n)")
                nc.scalar.activation(p32[:, k % 4, :], scores, ACT.Exp, bias=PROB_LIFT)
                need(act, pv_done, n - 3)
                nc.scalar.activation(p_hi[:, k % 4, :], scores, ACT.Exp, bias=PROB_LIFT).then_inc(exp_done, 1)

            with act.Fori(0, LEAD // 2 - 1) as p:
                for a in range(2):
                    for k in range(3):
                        tile_high(2 * p + a, k)
            for step in range(18):
                if step % 9 in (0, 3, 6):
                    tile_high(LEAD - 2 + step // 9, step % 9 // 3)

            def iteration(i, tiles, outs):
                T0 = 2 * i + LEAD
                P0 = 2 * (i - FIRST_OUTS)
                for step in range(32):
                    if tiles and step and tile_stage(step - 1):
                        a, part = tile_stage(step - 1)
                        if part % 3 == 0:
                            tile_high(T0 + a, part // 3)
                    if outs and step and out_stage(step - 1):
                        a, part = out_stage(step - 1)
                        if part == 0:
                            out_high(P0 + a)
                    exps(i, step)

            iteration(0, True, False)
            with act.Fori(1, FIRST_OUTS) as i:
                iteration(i, True, False)
            with act.Fori(FIRST_OUTS, LAST_TILES) as i:
                iteration(i, True, True)
            with act.Fori(LAST_TILES, ITERS - 1) as i:
                iteration(i, False, True)
            iteration(ITERS - 1, False, True)
            with act.Fori(ITERS - FIRST_OUTS, ITERS) as m:
                for a in range(2):
                    out_high(2 * m + a)

        @block.vector
        def _(dve):
            V = nc.vector
            V.memset(k_stack[96:98, :, :].bitcast(F32), 1.0).then_inc(s_const, 1)
            V.memset(v_parts[:, :, 0:1], 1.0).then_inc(s_const, 1)

            dve.wait_ge(s_small, 80)
            for c in range(NG, len(chunks)):
                kind, w, part, _ = chunks[c]
                dve.wait_ge(w_high, c + 1)
                bank = ps_st[:, (c % 4) // 2, c % 2, :].rearrange("p (c n) -> p c n", c=DC)
                both = wqkv_s[:, :, w] if kind == "w" else wp_s[:]
                rows = slice(part * 128, (part + 1) * 128)
                V.tensor_tensor(both[:, 1, :, rows], bank, both[:, 0, :, rows].bitcast(F32), ALU.subtract
                                ).then_inc(w_low, 1)
                if c == NG + 5:
                    dve.wait_ge(mod_ready, 1)
                    V.tensor_tensor(small4[0], ps_a[0:4, 0, :], small4[3], ALU.add).then_inc(gain_chain, 1)
                    V.tensor_tensor(small4[4], ps_a[0:4, 1, :], small4[4], ALU.add).then_inc(gain_chain, 1)
                    dve.wait_ge(gain_chain, 2)
                    V.tensor_tensor(small4[3], small4[0], small4[1], ALU.mult).then_inc(gain_chain, 1)
                    V.tensor_tensor(small4[2], small4[0], small4[2], ALU.mult).then_inc(gain_chain, 1)
                    dve.wait_ge(gain_chain, 4)
                    V.tensor_tensor(small4[4], small4[4], small4[2], ALU.add).then_inc(gain_chain, 1)

            def stats(rows, bn, mv, st, chain, count):
                V.bn_stats(bn, rows).then_inc(chain, 1)
                dve.drain()
                V.bn_aggr(mv, bn).then_inc(chain, 1)
                dve.wait_ge(chain, count + 2)
                V.tensor_scalar(st[:, 0:1], mv[:, 0:1], -1.0, None, ALU.mult)
                V.tensor_scalar(st[:, 1:2], mv[:, 1:2], EPS, None, ALU.add).then_inc(chain, 1)

            def tile_stats(pair, a):
                T = 2 * pair + a
                dve.wait_ge(x_in[a], 16 * pair + 16)
                need(dve, ln_pool, 4 * (T - 2) + 4)
                stats(x_tile[:, a, :], bn_t[:, a, :], mv_t[:, a, :], st_t[:, a, :], ln_stat, 3 * T)

            def tile_part(T, k):
                if k in (0, 3, 6):
                    dve.wait_ge(tile_hi, 3 * T + k // 3 + 1)
                    if k == 0:
                        high, low = (hT_s[:, e].rearrange("p c n -> p (c n)") for e in range(2))
                    else:
                        high, low = qkT_s[:, 2 * (k // 3) - 2, :], qkT_s[:, 2 * (k // 3) - 1, :]
                    V.tensor_tensor(low, ps_w[:], high.bitcast(F32), ALU.subtract).then_inc(tile_ev, 1)
                elif k in (2, 5):
                    dve.wait_ge(tile_mm, 6 * T + (2 if k == 2 else 4))
                    V.tensor_tensor(rows_t[:], ps_w[:], bq_s[:, :, k // 3], ALU.add).then_inc(tile_ev, 1)
                elif k == 8:
                    dve.wait_ge(tile_mm, 6 * T + 6)
                    dve.wait_ge(v_pool, 2 * T + ONE)
                    V.tensor_tensor(v_rest[:], ps_w[:], bq_s[:, :, 2], ALU.add).then_inc(tile_ev, 1)
                    dve.wait_ge(tile_ev, 6 * T + 6 + ONE)
                    dve.wait_ge(v_out, 16 * T + ONE)
                    V.tensor_copy(v_parts[:, :, 1:1 + HD], v_rest[:].rearrange("p (h d) -> p h d", h=H)).then_inc(v_dve, 1)

            def v_middle(T):
                dve.wait_ge(v_pool, 2 * T + 1 + ONE)
                V.tensor_copy(v_parts[:, :, 1 + HD:1 + 2 * HD], v_rest[:].rearrange("p (h d) -> p h d", h=H)
                              ).then_inc(v_dve, 1)

            def out_low(P):
                dve.wait_ge(out_hi, P + 1)
                V.tensor_tensor(oT_s[:, 1].rearrange("p c n -> p (c n)"), ps_w[:],
                                oT_s[:, 0].rearrange("p c n -> p (c n)").bitcast(F32), ALU.subtract).then_inc(out_ev, 1)

            def out_sum(pair, a):
                P = 2 * pair + a
                dve.wait_ge(out_mm, 2 * P + 2 + ONE)
                dve.wait_ge(res_ready, P + 1)
                dve.wait_ge(out_pool, 10 * pair + ONE)
                V.tensor_tensor(h1_t[:, a, :], ps_w[:], res_t[:, a, :], ALU.add).then_inc(out_ev, 1)

            def out_stats(P, a):
                dve.wait_ge(out_ev, 2 * P + 2 + ONE)
                stats(h1_t[:, a, :], obn_t[:, a, :], omv_t[:, a, :], ost_t[:, a, :], out_stat, 3 * P)

            def ring_item(s, item, m, parity):
                dve.wait_ge(a_ready, m + 1)
                V.tensor_reduce(half_max[:, s % 2, item:item + 1], ps_a[:, parity, :], AX.X, ALU.max).then_inc(a_used, 1)

            def ring_row(g, s, m, parity):
                dve.wait_ge(a_ready, m + 1)
                need(dve, row_in[s % 2], 64 * g + 32 * (s // 2))
                V.tensor_copy(max_rows[:, s % 2, :], ps_a[0:16, parity, 0:128]).then_inc(max_chain, 1)
                dve.wait_ge(max_chain, 16 * g + 4 * s + 4)
                dve.sem_inc(a_used, 1)

            def max_split(g, s, m_last):
                e = s % 2
                chain = 16 * g + 4 * s
                dve.wait_ge(a_used, m_last + 1)
                V.tensor_reduce(neg_max[:, e, :], half_max[:, e, :].rearrange("p (t h) -> p t h", h=2), AX.X, ALU.max,
                                negate=True).then_inc(max_chain, 1)
                dve.wait_ge(max_chain, chain + 1)
                V.tensor_copy(max_parts[:, e, 0:8], neg_max[:, e, :]).then_inc(max_chain, 1)
                dve.wait_ge(max_chain, chain + 2)
                V.tensor_tensor(max_parts[:, e, 8:16], neg_max[:, e, :], max_parts[:, e, 0:8].bitcast(F32), ALU.subtract
                                ).then_inc(max_chain, 1)

            def low(i, step):
                n, k = 32 * i + step, step % 8
                dve.wait_ge(exp_done, n + 1)
                need(dve, pv_done, n - 3)
                V.tensor_tensor(p_lo[:, k % 4, :], p32[:, k % 4, :], p_hi[:, k % 4, :], ALU.subtract).then_inc(lo_even, 1)

            def normalise(g, s, half):
                v = 4 * g + s
                chain = 3 * (2 * v + half)
                dve.wait_ge(pv_done, 8 * v + 4 * half + 4)
                V.tensor_reduce(o_sum[:], ps_o[:, :, 1:VP].rearrange("p t (c d) -> p t d c", c=3), AX.X, ALU.add
                                ).then_inc(o_chain, 1)
                V.reciprocal(o_rcp[:], ps_o[:, :, 0]).then_inc(o_chain, 1)
                dve.wait_ge(o_chain, chain + 2)
                need(dve, att_out[half], 16 * v)
                V.scalar_tensor_tensor(out=o_out[:, half, :, :], in0=o_sum[:], scalar=ATT_SCALE,
                                       in1=o_rcp[:].unsqueeze(2).to_broadcast([128, 4, HD]),
                                       op0=ALU.mult, op1=ALU.mult).then_inc(o_chain, 1)

            for a in range(2):
                tile_stats(0, a)
            dve.wait_ge(s_bias, 32)
            with dve.Fori(0, LEAD // 2 - 1) as p:
                for a in range(2):
                    T = 2 * p + a
                    for k in range(9):
                        tile_part(T, k)
                    tile_stats(p + 1, a)
                    v_middle(T)
            for step in range(21):
                for m in range(*LEAD_SPAN.get(step, (0, 0))):
                    v, item = lead_item(m)
                    if item == 16:
                        ring_row(0, v, m, m % 2)
                    else:
                        ring_item(v, item, m, m % 2)
                    if (v, item) == (0, 15):
                        max_split(0, 0, m)
                if 1 <= step <= 18:
                    T = LEAD - 2 + (step - 1) // 9
                    tile_part(T, (step - 1) % 9)
                if step in (11, 20):
                    v_middle(LEAD - 2 + (step - 10) // 9)

            def iteration(i, tiles, outs, first=False, last=False):
                T0 = 2 * i + LEAD
                pair = i - FIRST_OUTS
                for s in range(4):
                    u = 4 * i + s
                    for k in range(8):
                        step = 8 * s + k
                        if k == 2 and not (first and s == 0):
                            normalise(i - (s == 0), (s - 1) % 4, 1)
                        if k == 6:
                            normalise(i, s, 0)
                        for g, sa, item, m, parity in ring_uses(i, s, k, last):
                            if item == 16:
                                ring_row(g, sa, m, parity)
                            else:
                                ring_item(sa, item, m, parity)
                            if item == 15:
                                max_split(g, sa, m)
                        if tiles and step and tile_stage(step - 1):
                            a, part = tile_stage(step - 1)
                            tile_part(T0 + a, part)
                        if outs and step and out_stage(step - 1):
                            a, part = out_stage(step - 1)
                            if part == 0:
                                out_low(2 * pair + a)
                            if part == 2:
                                out_sum(pair, a)
                        if k % 2 == 0:
                            low(i, step)
                        for a in range(2):
                            if tiles and step == LN_STEP[a]:
                                tile_stats(i + LEAD // 2, a)
                            if tiles and step == TILE_STEP[a] + 11:
                                v_middle(T0 + a)
                            if outs and step == OUT_STEP[a] + 4:
                                out_stats(2 * pair + a, a)

            iteration(0, True, False, first=True)
            with dve.Fori(1, FIRST_OUTS) as i:
                iteration(i, True, False)
            with dve.Fori(FIRST_OUTS, LAST_TILES) as i:
                iteration(i, True, True)
            with dve.Fori(LAST_TILES, ITERS - 1) as i:
                iteration(i, False, True)
            iteration(ITERS - 1, False, True, last=True)
            normalise(ITERS - 1, 3, 1)
            with dve.Fori(ITERS - FIRST_OUTS, ITERS) as m:
                for a in range(2):
                    out_low(2 * m + a)
                    out_sum(m, a)
                    out_stats(2 * m + a, a)

        @block.gpsimd
        def _(pool):
            G = nc.gpsimd
            for semaphore in start_at_one:
                pool.sem_inc(semaphore, ONE)
            G.memset(minus_half[:], -0.5)
            G.memset(ident[:], 0.0).then_inc(id_zero, 1)
            pool.wait_ge(id_zero, 1)
            G.affine_select(out=ident[:], in_=ident[:], compare_op=ALU.not_equal, fill=1.0, base=0,
                            pattern=[[-1, 128]], channel_multiplier=1).then_inc(s_const, 1)

            def power(st, chain, count):
                G.tensor_tensor(st[:, 2:3], st[:, 1:2], minus_half[:], ALU.pow).then_inc(chain, 1)
                pool.drain()

            def norm(pair, a):
                T = 2 * pair + a
                pool.wait_ge(ln_stat, 3 * T + 3)
                need(pool, tile_mm, 6 * (T - 2) + 1)
                power(st_t[:, a, :], ln_pool, 4 * T)
                h = h_tile[:, a, :]
                G.tensor_scalar(h, x_tile[:, a, :], st_t[:, a, 0:1], st_t[:, a, 2:3], ALU.add, ALU.mult).then_inc(ln_pool, 1)
                pool.wait_ge(ln_pool, 4 * T + 2)
                pool.wait_ge(gq_in, 16 * pair + 16)
                G.tensor_tensor(h, h, gq_s[:, 0, :], ALU.mult).then_inc(ln_pool, 1)
                pool.wait_ge(ln_pool, 4 * T + 3)
                G.tensor_tensor(h, h, gq_s[:, 1, :], ALU.add).then_inc(ln_pool, 1)

            def v_take_high(T):
                pool.wait_ge(v_dve, 2 * T + 1)
                rest = v_rest[:].rearrange("p (h d) -> p h d", h=H)
                G.tensor_tensor(rest, rest, v_parts[:, :, 1:1 + HD], ALU.subtract).then_inc(v_pool, 1)

            def v_take_middle(T):
                pool.wait_ge(v_dve, 2 * T + 2)
                rest = v_rest[:].rearrange("p (h d) -> p h d", h=H)
                G.tensor_tensor(v_parts[:, :, 1 + 2 * HD:VP], rest, v_parts[:, :, 1 + HD:1 + 2 * HD], ALU.subtract
                                ).then_inc(v_pool, 1)

            def residual(pair, a):
                pool.wait_ge(res_in[a], 16 * pair + 16)
                G.tensor_tensor(res_t[:, a, :], res_t[:, a, :], bp_s[:], ALU.add).then_inc(res_ready, 1)

            def out_norm(pair, a):
                P = 2 * pair + a
                count = 5 * P + ONE
                pool.wait_ge(out_stat, 3 * P + 3)
                power(ost_t[:, a, :], out_pool, count)
                y = y_t[:, a, :]
                G.tensor_scalar(y, h1_t[:, a, :], ost_t[:, a, 0:1], ost_t[:, a, 2:3], ALU.add, ALU.mult).then_inc(out_pool, 1)
                pool.wait_ge(out_pool, count + 2)
                pool.wait_ge(go_in, 16 * pair + 16)
                G.tensor_tensor(y, y, go_s[:, 0, :], ALU.mult).then_inc(out_pool, 1)
                pool.wait_ge(out_pool, count + 3)
                G.tensor_tensor(y, y, go_s[:, 1, :], ALU.add).then_inc(out_pool, 1)
                pool.wait_ge(out_pool, count + 4)
                G.tensor_tensor(y, y, h1_t[:, a, :], ALU.add).then_inc(out_pool, 1)
                pool.wait_ge(out_pool, count + 5)
                G.dma_start(out_rows[bass.ds(P * 128, 128), :], y).then_inc(y_out[a], 16)
                if a == 1:
                    for e in range(2):
                        pool.wait_ge(y_out[e], 16 * pair + 16)

            def low(i, step):
                n, k = 32 * i + step, step % 8
                pool.wait_ge(exp_done, n + 1)
                need(pool, pv_done, n - 3)
                G.tensor_tensor(p_lo[:, k % 4, :], p32[:, k % 4, :], p_hi[:, k % 4, :], ALU.subtract).then_inc(lo_odd, 1)

            pool.wait_ge(s_bias, 32)
            norm(0, 0)
            norm(0, 1)
            with pool.Fori(0, LEAD // 2 - 1) as p:
                for a in range(2):
                    v_take_high(2 * p + a)
                    norm(p + 1, a)
                    v_take_middle(2 * p + a)
            for a in range(2):
                v_take_high(LEAD - 2 + a)
                v_take_middle(LEAD - 2 + a)

            def iteration(i, tiles, outs):
                T0 = 2 * i + LEAD
                pair = i - FIRST_OUTS
                for step in range(32):
                    if step % 2:
                        low(i, step)
                    for a in range(2):
                        if tiles and step == LN_STEP[a] + 1:
                            norm(i + LEAD // 2, a)
                        if tiles and step == TILE_STEP[a] + 10:
                            v_take_high(T0 + a)
                        if tiles and step == TILE_STEP[a] + 12:
                            v_take_middle(T0 + a)
                        if outs and step == 21 + a:
                            residual(pair, a)
                        if outs and step == (29, 31)[a]:
                            out_norm(pair, a)

            iteration(0, True, False)
            with pool.Fori(1, FIRST_OUTS) as i:
                iteration(i, True, False)
            with pool.Fori(FIRST_OUTS, LAST_TILES) as i:
                iteration(i, True, True)
            with pool.Fori(LAST_TILES, ITERS - 1) as i:
                iteration(i, False, True)
            iteration(ITERS - 1, False, True)
            with pool.Fori(ITERS - FIRST_OUTS, ITERS) as m:
                for a in range(2):
                    residual(m, a)
                for a in range(2):
                    out_norm(m, a)


NAMES = ["x", "cond_1024"] + ["L0_cond_" + n for n in (
    "ln_g", "ln_b", "Wg", "bg", "Wb", "bb", "Wqkv", "bqkv", "Wp", "bp")]


def kernel(**inputs):
    import numpy as np
    import concourse.bacc as bacc
    from concourse.bass_utils import run_bass_kernel_spmd

    nc = bacc.Bacc("TRN2", target_bir_lowering=False, num_devices=1)
    arrays, args = {}, []
    for name in NAMES:
        a = np.ascontiguousarray(inputs[name])
        arrays[f"in_{name}"] = a
        args.append(nc.dram_tensor(f"in_{name}", a.shape, mybir.dt.from_np(a.dtype), kind="ExternalInput").ap())
    out = nc.dram_tensor("out_y", inputs["x"].shape, F32, kind="ExternalOutput").ap()
    conditioned_attention(nc, *args, out)
    result = run_bass_kernel_spmd(nc, [arrays], core_ids=[0])
    return result.results[0]["out_y"]
```

```python
from contextlib import ExitStack

import concourse.bass as bass
from concourse import mybir

ALU = mybir.AluOpType
ACT = mybir.ActivationFunctionType
AX = mybir.AxisListType
F32 = mybir.dt.float32
FR = mybir.dt.float32r
F16 = mybir.dt.float16
BF16 = mybir.dt.bfloat16

EPS = 1e-05
PROB_LIFT = 8.0

SPLIT = [(0, 0), (0, 1), (1, 0)]

PAIR_STAGE = {0: (0, 0), 2: (1, 0), 4: (2, 0), 5: (2, 1), 7: (3, 0), 8: (3, 1), 10: (4, 0), 11: (4, 1),
              13: (5, 0), 14: (5, 1), 16: (6, 0), 17: (6, 1), 19: (7, 0), 20: (7, 1)}
OUT_STAGE = {22: (0, 0), 24: (0, 1), 25: (0, 2), 27: (1, 0), 29: (1, 1), 30: (1, 2)}
LN_STEP = {5: 0, 13: 1}
V_MIDDLE_STEP = {22: 0, 24: 1}
OUT_STATS_STEP = {27: 0, 31: 1}
POOL_LOW = {2, 10, 18, 26} | set(range(1, 32, 2))
DVE_LOW_EARLY = {8, 16, 24, 28}
SUM_LAG = 3


def conditioned_attention(nc, x, cond, ln_g, ln_b, Wg, bg, Wb, bb, Wqkv, bqkv, Wp, bp, out):
    B, N, D = x.shape
    HD = 32
    H = D // HD
    DC = D // 128
    NV = B * H
    NT = B * N // 128
    ITERS = NV // 4
    PAIRS = NT // 2
    LEAD = N // 256 + 1
    VP = 3 * HD + 1
    NL = 2 * HD + 1
    ATT_SCALE = float(D) ** -0.5
    LAST_TILES = PAIRS - LEAD
    FIRST_OUTS = H // 4

    x_rows = x.rearrange("b n d -> (b n) d")
    out_rows = out.rearrange("b n d -> (b n) d")
    qk_d = nc.dram_tensor("qk_scratch", [4, B, D, N], F32, kind="Internal").ap()
    v_d = nc.dram_tensor("v_scratch", [NV, 128, N // 128, VP], BF16, kind="Internal").ap()
    att_d = nc.dram_tensor("att_scratch", [B * N, D], F32, kind="Internal").ap()
    gb_d = nc.dram_tensor("gain_bias_scratch", [PAIRS, 2, D], F32, kind="Internal").ap()
    mark_d = nc.dram_tensor("mark_scratch", [2, 1, 16], F32, kind="Internal").ap()
    att_heads = att_d.rearrange("(b e t p) (h d) -> b h e p t d", b=B, e=2, p=128, d=HD)
    qk_heads = qk_d.rearrange("w b (h d) n -> w (b h) d n", d=HD)
    qk_pairs = qk_d.rearrange("w b (c p) (t n) -> w b t p c n", p=128, n=256)
    v_tiles = v_d.rearrange("(b h) p t c -> b t p h c", b=B)

    with ExitStack() as ctx:
        def sb(name, shape, dt=F32):
            return ctx.enter_context(nc.sbuf_tensor(name, shape, dt))

        def sem(name):
            return ctx.enter_context(nc.semaphore(name))

        ps_st = ctx.enter_context(nc.psum_tensor("ps_st", [128, 2, 2, 512], F32))
        ps_a = ctx.enter_context(nc.psum_tensor("ps_a", [128, 2, 512], F32))
        ps_o = ctx.enter_context(nc.psum_tensor("ps_o", [128, 4, 128], F32))
        ps_w = ctx.enter_context(nc.psum_tensor("ps_w", [128, 512], F32))

        ident = sb("ident", [128, 128])
        wqkv_s = sb("wqkv_s", [128, 2, 3, DC, 512], FR)
        wp_s = sb("wp_s", [128, 2, DC, 512], FR)
        zero_s = sb("zero_s", [128, 1])
        eps_s = sb("eps_s", [128, 1])
        minus_half = sb("minus_half", [128, 1])
        bqk_s = sb("bqk_s", [128, DC, 3])
        bv_s = sb("bv_s", [128, D])
        bp_s = sb("bp_s", [128, D])
        gq_s = sb("gq_s", [128, 2, D])
        go_s = sb("go_s", [128, 2, D])
        q_stack = sb("q_stack", [128, 4, N], FR)
        k_stack = sb("k_stack", [128, 4, N], FR)
        v_head = sb("v_head", [128, 4, N // 128, VP], BF16)
        p32 = sb("p32", [128, 4, 1024])
        p_hi = sb("p_hi", [128, 4, 1024], F16)
        p_lo = sb("p_lo", [128, 4, 1024], F16)
        half_max = sb("half_max", [128, 2, 16])
        neg_max = sb("neg_max", [128, 2, 8])
        max_parts = sb("max_parts", [128, 2, 16], FR)
        max_rows = sb("max_rows", [16, 2, 128], FR)
        o_sum = sb("o_sum", [128, 4, HD])
        o_rcp = sb("o_rcp", [128, 4])
        o_out = sb("o_out", [128, 2, 4, HD])
        x_tile = sb("x_tile", [128, 2, D])
        h_tile = sb("h_tile", [128, 2, D])
        bn_t = sb("bn_t", [128, 2, 6])
        mv_t = sb("mv_t", [128, 2, 2])
        std_t = sb("std_t", [128, 2, 2])
        hT_s = sb("hT_s", [128, 2, DC, 256], FR)
        qkT_s = sb("qkT_s", [128, 2, 2, 512], FR)
        v_rest = sb("v_rest", [128, 2, 512])
        v_parts = sb("v_parts", [128, 2, H, VP], BF16)
        att_t = sb("att_t", [128, 2, D])
        res_t = sb("res_t", [128, 2, D])
        oT_s = sb("oT_s", [128, 2, DC, 128], FR)
        h1_t = sb("h1_t", [128, 2, D])
        y_t = sb("y_t", [128, 2, D])
        obn_t = sb("obn_t", [128, 2, 6])
        omv_t = sb("omv_t", [128, 2, 2])
        ostd_t = sb("ostd_t", [128, 2, 2])
        small4 = [att_t[0:4, 0, :], att_t[0:4, 1, :], h1_t[0:4, 0, :], res_t[0:4, 0, :], res_t[0:4, 1, :]]
        condT = sb("condT", [128, DC, 4])

        id_ready = sem("id_ready")
        ones_set = sem("ones_set")
        id_zero = sem("id_zero")
        s_small = sem("s_small")
        s_bias = sem("s_bias")
        bv_ready = sem("bv_ready")
        raw_in = [sem(f"raw_in{r}") for r in range(8)]
        w_turned = sem("w_turned")
        w_high = sem("w_high")
        w_low = sem("w_low")
        cond_turned = sem("cond_turned")
        cond_ready = sem("cond_ready")
        mod_ready = sem("mod_ready")
        gain_chain = sem("gain_chain")
        gain_stored = sem("gain_stored")
        qk_in = [sem(f"qk_in{s}") for s in range(4)]
        v_in = [sem(f"v_in{s}") for s in range(4)]
        row_in = [sem(f"row_in{s}") for s in range(2)]
        a_ready = sem("a_ready")
        a_used = sem("a_used")
        max_chain = sem("max_chain")
        st_ready = sem("st_ready")
        exp_done = sem("exp_done")
        low_dve = sem("low_dve")
        low_pool = sem("low_pool")
        pv_done = sem("pv_done")
        o_chain = sem("o_chain")
        att_out = [sem(f"att_out{s}") for s in range(2)]
        x_in = [sem(f"x_in{s}") for s in range(2)]
        gq_in = sem("gq_in")
        ln_stat = sem("ln_stat")
        ln_pool = sem("ln_pool")
        tile_mm = sem("tile_mm")
        tile_hi = sem("tile_hi")
        tile_ev = sem("tile_ev")
        v_dve = sem("v_dve")
        v_pool = sem("v_pool")
        qk_out = [sem(f"qk_out{s}") for s in range(2)]
        v_out = [sem(f"v_out{a}") for a in range(2)]
        att_in = [sem(f"att_in{s}") for s in range(2)]
        res_in = [sem(f"res_in{s}") for s in range(2)]
        go_in = sem("go_in")
        res_ready = sem("res_ready")
        out_turned = sem("out_turned")
        out_hi = sem("out_hi")
        out_lo = sem("out_lo")
        out_projected = sem("out_projected")
        out_summed = sem("out_summed")
        out_stat = sem("out_stat")
        out_pool = sem("out_pool")
        y_out = [sem(f"y_out{s}") for s in range(2)]
        last_std = sem("last_std")
        last_chain = sem("last_chain")
        last_out = sem("last_out")
        ONE = 1
        start_at_one = [*qk_out, *v_out, v_pool, out_turned, out_lo, out_summed, out_pool, last_chain, last_out]
        PAIR_BEFORE = 8

        def need(eng, semaphore, value):
            if not isinstance(value, int) or value > 0:
                eng.wait_ge(semaphore, value)

        wqkv_rows = Wqkv.rearrange("(j c) d -> c j d", c=3)
        chunks = [("g", 0, c, Wg[c * 128:(c + 1) * 128, :]) for c in range(DC)]
        chunks += [("g", 1, c, Wb[c * 128:(c + 1) * 128, :]) for c in range(DC)]
        chunks += [("w", w, c, wqkv_rows[w, c * 128:(c + 1) * 128, :]) for w in range(3) for c in range(DC)]
        chunks += [("p", 0, c, Wp[c * 128:(c + 1) * 128, :]) for c in range(DC)]
        NG = 2 * DC
        raw_slot = [half[:].rearrange("p a n -> p (a n)").bitcast(F32)[:, r * 512:(r + 1) * 512]
                    for half in (p_hi, p_lo) for r in range(4)]
        bias_stage = [buf[:].rearrange("p a d -> p (a d)")[:, 0:3 * D // 2] for buf in (h_tile, v_rest)]
        modT = p32[:].rearrange("p a (b n) -> p (a b) n", n=512)

        A_LEAD = 16 + 8 + 1

        def lead_item(k):
            return ([(0, q) for q in range(16)] + [(1, q) for q in range(4)] + [(0, 16)]
                    + [(1, q) for q in range(4, 8)])[k]

        LEAD_STAGE = dict(enumerate([(0, 0), (1, 0)] + [(f, part) for f in range(2, 8) for part in range(2)]))
        LEAD_STEPS = 16
        LEAD_SPAN = {s + 3: (2 * s, 2 * s + 2) for s in range(9)} | {
            12: (18, 20), 13: (20, 21), 14: (21, 23), 15: (23, 25)}

        def ring_items(k):
            if k < 4:
                return [(2 * k, 1, 8 + 2 * k), (2 * k + 1, 1, 9 + 2 * k)]
            items = {4: [(8, 2, 0), (9, 2, 1)], 5: [(10, 1, 16), (11, 2, 2), (12, 2, 3)],
                     6: [(13, 2, 4), (14, 2, 5)], 7: [(15, 2, 6), (16, 2, 7)]}
            return items[k]

        def ring_uses(i, s, k, last):
            uses = []
            for pos, ahead, item in ring_items(k):
                if last and s + ahead > 3:
                    continue
                gone = 2 if last and s == 2 and item == 16 else 0
                uses.append((i + (s + ahead) // 4, (s + ahead) % 4, item,
                             A_LEAD + 17 * (4 * i + s) + pos - gone, (A_LEAD + 17 * s + pos) % 2))
            return uses

        pool_lows = sum(step in POOL_LOW for step in range(32))

        def low_count(i, step):
            i, step = i + step // 32, step % 32
            by_pool = step in POOL_LOW
            upto = sum((n in POOL_LOW) == by_pool for n in range(step + 1))
            return (low_pool, pool_lows * i + upto) if by_pool else (low_dve, (32 - pool_lows) * i + upto)

        def evacuated(stages, step):
            stage = stages.get(step - 1)
            return stage[0] if stage and (stage[1] == 1 or stage[0] < 2) else None

        LEAD_BANK = [ps_st[:, 0, 0, :], ps_st[:, 0, 1, :], ps_st[:, 1, 0, :], ps_st[:, 1, 1, :],
                     ps_st[:, 0, 0, :], ps_st[:, 0, 1, :], ps_w[:], ps_o[:].rearrange("p t c -> p (t c)")]
        LEAD_BEFORE = [4 - 8, 5 - 8, 2 - 8, 3 - 8, 0, 1, 6 - 8, 7 - 8]

        def bank_of(fill, lead):
            return LEAD_BANK[fill] if lead else ps_w[:]

        def qk_slot(fill, part, lead):
            if lead and fill > 3:
                return p32[:, fill - 2, part * 512:(part + 1) * 512].bitcast(FR)
            return qkT_s[:, fill % 2, part, :]

        def turned_bank(a, end):
            return ps_st[:, 0, a, :] if end else ps_w[:]

        def turned_rows(a, end):
            return hT_s[:, :, :, a * 128:(a + 1) * 128] if end else oT_s[:]

        def projected_bank(a, end):
            return ps_a[:, a, :] if end else ps_w[:]

        block = ctx.enter_context(nc.Block())

        @block.sync
        def _(sp):
            for r in range(8):
                sp.dma_start(raw_slot[r], chunks[r][3]).then_inc(raw_in[r], 16)
            sp.dma_start(small4[0], cond).then_inc(s_small, 16)
            for slot, row in ((1, ln_g), (2, ln_b), (3, bg), (4, bb)):
                sp.dma_start(small4[slot], row.rearrange("(a d) -> a d", a=1).to_broadcast([4, D])
                             ).then_inc(s_small, 16)
            sp.dma_start(bp_s[:], bp.rearrange("(a d) -> a d", a=1).to_broadcast([128, D])).then_inc(s_bias, 16)
            for half in range(2):
                sp.dma_start(bias_stage[half], bqkv.rearrange("(h d) -> h d", h=2)[half:half + 1].to_broadcast(
                    [128, 3 * D // 2])).then_inc(s_bias, 16)
            sp.dma_start(bqk_s[:], bqkv.rearrange("(c p w) -> p c w", p=128, w=3)).then_inc(s_bias, 16)
            for a in range(2):
                sp.dma_start(x_tile[:, a, :], x_rows[a * 128:(a + 1) * 128, :]).then_inc(x_in[a], 16)
            for c in range(8, len(chunks)):
                sp.wait_ge(w_turned, c - 7)
                sp.dma_start(raw_slot[c % 8], chunks[c][3]).then_inc(raw_in[c % 8], 16)
            sp.wait_ge(gain_chain, 5)
            batches = gb_d.rearrange("(b r) c d -> r b c d", b=B)
            for r in range(PAIRS // B):
                sp.dma_start(batches[r], res_t[0:4, :, :]).then_inc(gain_stored, 16)
            sp.wait_ge(gain_stored, 16 * (PAIRS // B))

            def at_tile(tiles, T):
                per = N // 128
                part = tiles[bass.ds(T // per, 1), bass.ds(T % per, 1)]
                return part.rearrange("b t p c n -> (b t p) c n")

            def load_x(pair, a):
                sp.dma_start(x_tile[:, a, :], x_rows[bass.ds((2 * pair + a) * 128, 128), :]).then_inc(x_in[a], 16)

            def load_gain(dst, dst_sem, pair):
                src = gb_d[bass.ds(pair, 1), :, :].rearrange("a c d -> a (c d)")
                sp.dma_start(dst[:].rearrange("p c d -> p (c d)"),
                             src.to_broadcast([128, 2 * D])).then_inc(dst_sem, 16)

            def store_rows(pair, fill, lead=False):
                w, half = (fill - 2) // 2, fill % 2
                per = N // 256
                sp.wait_ge(tile_ev, 8 * pair + fill + 1 + PAIR_BEFORE)
                for part in range(2):
                    dst = qk_pairs[2 * w + part, bass.ds(pair // per, 1), bass.ds(pair % per, 1), :, 2 * half:2 * half + 2, :]
                    sp.dma_start(dst.rearrange("b t p c n -> (b t p) c n"),
                                 qk_slot(fill, part, lead).bitcast(F32).rearrange("p (c n) -> p c n", n=256)
                                 ).then_inc(qk_out[half], 16)

            def store_v(pair, a):
                sp.wait_ge(v_pool, 4 * pair + 3 + a + ONE)
                sp.dma_start(at_tile(v_tiles, 2 * pair + a), v_parts[:, a]).then_inc(v_out[a], 16)

            def wait_pairs(pairs):
                for s in range(2):
                    sp.wait_ge(qk_out[s], 64 * pairs + ONE)
                    sp.wait_ge(v_out[s], 16 * pairs + ONE)

            def load_stacks(v, s):
                for row, part in ((0, 0), (1, 0), (2, 1)):
                    sp.dma_start(q_stack[row * HD:(row + 1) * HD, s, :].bitcast(F32),
                                 qk_heads[part, bass.ds(v, 1)].rearrange("a d n -> (a d) n")).then_inc(qk_in[s], 16)
                for row, part in ((0, 2), (1, 3), (2, 2)):
                    sp.dma_start(k_stack[row * HD:(row + 1) * HD, s, :].bitcast(F32),
                                 qk_heads[part, bass.ds(v, 1)].rearrange("a d n -> (a d) n")).then_inc(qk_in[s], 16)

            def load_v(v, s):
                sp.dma_start(v_head[:, s, :, :], v_d[bass.ds(v, 1)].rearrange("a p t c -> (a p) t c")
                             ).then_inc(v_in[s], 16)

            def store_row(v, s):
                sp.wait_ge(max_chain, 4 * v + 4)
                for part in range(2):
                    sp.dma_start(q_stack[96 + part:97 + part, s, :].bitcast(F32),
                                 max_rows[8 * part:8 * part + 8, s % 2, :].bitcast(F32)).then_inc(row_in[s % 2], 16)

            def store_att(v, half):
                sp.wait_ge(o_chain, 3 * (2 * v + half) + 3)
                sp.dma_start(att_heads[bass.ds(v // H, 1), bass.ds(v % H, 1), half].rearrange("b h p t d -> (b h p) t d"),
                             o_out[:, half, :, :]).then_inc(att_out[half], 16)

            def load_out(pair, a):
                sp.wait_ge(out_turned, 2 * pair - 1 + a + ONE if a else 2 * pair + ONE)
                sp.dma_start(att_t[:, a, :], att_d[bass.ds((2 * pair + a) * 128, 128), :]).then_inc(att_in[a], 16)
                sp.wait_ge(out_summed, 2 * pair - 1 + a + ONE if a else 2 * pair + ONE)
                sp.dma_start(res_t[:, a, :], x_rows[bass.ds((2 * pair + a) * 128, 128), :]).then_inc(res_in[a], 16)

            def store_last(m):
                sp.wait_ge(last_chain, 3 * (m - (ITERS - FIRST_OUTS)) + 3 + ONE)
                sp.dma_start(out_rows[bass.ds((2 * m + 1) * 128, 128), :], y_t[:, 1, :]).then_inc(last_out, 16)

            load_gain(gq_s, gq_in, 0)
            sp.wait_ge(ln_pool, 8)
            load_gain(gq_s, gq_in, 1)
            for a in range(2):
                load_x(1, a)
            with sp.Fori(0, LEAD - 1) as p:
                for fill in range(2, 6):
                    store_rows(p, fill, lead=True)
                sp.wait_ge(ln_pool, 8 * p + 16)
                load_gain(gq_s, gq_in, p + 2)
                for a in range(2):
                    load_x(p + 2, a)
                for a in range(2):
                    store_v(p, a)
            wait_pairs(LEAD - 1)
            for v in range(3):
                load_stacks(v, v)
                load_v(v, v)
            for fill in range(2, 6):
                store_rows(LEAD - 1, fill, lead=True)
            store_row(0, 0)
            for a in range(2):
                store_v(LEAD - 1, a)

            def iteration(i, tiles, norms, outs, first=False, last=False):
                pair = i - FIRST_OUTS
                for s in range(4):
                    u = 4 * i + s
                    for k in range(8):
                        step = 8 * s + k
                        if step == 0:
                            if norms:
                                sp.wait_ge(ln_pool, 8 * (i + LEAD + 1))
                                load_gain(gq_s, gq_in, i + LEAD + 1)
                                for a in range(2):
                                    load_x(i + LEAD + 1, a)
                            wait_pairs(i + LEAD if tiles else PAIRS)
                        if k == 0 and not (first and s == 0):
                            store_att(u - 1, 0)
                        if k == 1 and not (last and s > 0):
                            need(sp, st_ready, 8 * u)
                            load_stacks(u + 3, (s + 3) % 4)
                        if k == 4 and not (first and s == 0):
                            store_att(u - 1, 1)
                        if k == 4 and not (last and s > 0):
                            need(sp, pv_done, 8 * u)
                            load_v(u + 3, (s + 3) % 4)
                        if k == 6 and not (last and s == 3):
                            store_row(u + 1, (s + 1) % 4)
                        if outs and step == 8:
                            sp.wait_ge(out_pool, 10 * pair + ONE)
                            load_gain(go_s, go_in, pair)
                            for half in range(2):
                                sp.wait_ge(att_out[half], 64 * i)
                            for a in range(2):
                                load_out(pair, a)
                        if tiles:
                            for fill in range(2, 6):
                                if evacuated(PAIR_STAGE, step - 2) == fill:
                                    store_rows(i + LEAD, fill)
                            if step in (24, 26):
                                store_v(i + LEAD, step // 2 - 12)

            iteration(0, True, True, False, first=True)
            with sp.Fori(1, FIRST_OUTS) as i:
                iteration(i, True, True, False)
            with sp.Fori(FIRST_OUTS, LAST_TILES - 1) as i:
                iteration(i, True, True, True)
            iteration(LAST_TILES - 1, True, False, True)
            with sp.Fori(LAST_TILES, ITERS - 1) as i:
                iteration(i, False, False, True)
            iteration(ITERS - 1, False, False, True, last=True)
            for half in range(2):
                store_att(NV - 1, half)
            sp.wait_ge(out_pool, 10 * (ITERS - FIRST_OUTS) + ONE)
            load_gain(go_s, go_in, ITERS - FIRST_OUTS)
            for half in range(2):
                sp.wait_ge(att_out[half], 16 * NV)
            for a in range(2):
                load_out(ITERS - FIRST_OUTS, a)
            with sp.Fori(ITERS - FIRST_OUTS, ITERS - 1) as m:
                for a in range(2):
                    load_out(m + 1, a)
                store_last(m)
            store_last(ITERS - 1)
            for a in range(2):
                sp.wait_ge(y_out[a], 16 * (1 + PAIRS - a * FIRST_OUTS))
            sp.wait_ge(last_out, 16 * FIRST_OUTS + ONE)

        @block.tensor
        def _(pe):
            f_ident = ident[:]

            def split_product(dst, left, right, count=range(12)):
                for n in count:
                    c, (lp, rp) = n // 3, SPLIT[n % 3]
                    mm = pe.matmul(dst, left[:, lp, c, :], right[:, rp, c, :], start=(n == 0), stop=(n == 11))
                return mm

            pe.wait_ge(id_ready, 1)
            for c in range(len(chunks)):
                pe.wait_ge(raw_in[c % 8], 16 * (c // 8 + 1))
                if c >= 4:
                    if c - 4 < NG:
                        pe.wait_ge(w_high, c - 3)
                    else:
                        pe.wait_ge(w_low, c - 3 - NG)
                bank = ps_st[:, (c % 4) // 2, c % 2, :]
                for d in range(DC):
                    mm = pe.transpose(bank[:, d * 128:(d + 1) * 128], raw_slot[c % 8][:, d * 128:(d + 1) * 128], f_ident)
                mm.then_inc(w_turned, 1)
                if c == NG:
                    pe.wait_ge(s_small, 80)
                    for d in range(DC):
                        mm = pe.transpose(ps_w[:, d * 4:d * 4 + 4], small4[0][:, d * 128:(d + 1) * 128], f_ident[0:4, 0:4])
                    mm.then_inc(cond_turned, 1)
                if c == NG + 4:
                    pe.wait_ge(cond_ready, 1)
                    for m in range(2):
                        for d in range(DC):
                            mm = pe.matmul(ps_a[0:4, m, :], condT[:, d, :],
                                           modT[:, m * DC + d, :], start=(d == 0), stop=(d == DC - 1))
                    mm.then_inc(mod_ready, 1)

            def stage(pair, fill, part, lead=False, piece=None):
                bank = bank_of(fill, lead)
                if fill < 2 and piece == 1:
                    return
                passes = range(6) if piece is None else range(3 * piece, 3 * piece + 3)
                ends = piece != 0
                if part == 0 and piece != 1:
                    before = LEAD_BEFORE[fill] if lead else fill - 1
                    pe.wait_ge(tile_ev, 8 * pair + before + 1 + PAIR_BEFORE)
                if fill < 2:
                    pe.wait_ge(ln_pool, 8 * pair + 4 * fill + 4)
                    for d in range(DC):
                        mm = pe.transpose(bank[:, d * 128:(d + 1) * 128], h_tile[:, fill, d * 128:(d + 1) * 128], f_ident)
                    mm.then_inc(tile_mm, 1)
                    return
                if fill == 2 and part == 0 and piece != 1:
                    pe.wait_ge(tile_ev, 8 * pair + 2 + PAIR_BEFORE)
                if fill < 6:
                    w, chunk = (fill - 2) // 2, 2 * (fill % 2) + part
                    for n in [n for p in passes for n in (2 * p, 2 * p + 1)]:
                        d, (lp, rp) = n // 3, SPLIT[n % 3]
                        mm = pe.matmul(bank[:, part * 256:(part + 1) * 256],
                                       wqkv_s[:, lp, w, d, chunk * 128:(chunk + 1) * 128], hT_s[:, rp, d, :],
                                       start=(n == 0), stop=(n == 11))
                else:
                    tokens = slice((fill - 6) * 128, (fill - 5) * 128)
                    mm = split_product(bank, hT_s[:, :, :, tokens], wqkv_s[:, :, 2], [6 * part + p for p in passes])
                if part == 1 and ends:
                    mm.then_inc(tile_mm, 1)

            def out_part(pair, a, k, end=False, piece=None):
                P = 2 * pair + a
                if k == 0 and piece == 1:
                    return
                passes = range(6) if piece is None else range(3 * piece, 3 * piece + 3)
                if k == 0:
                    pe.wait_ge(att_in[a], 16 * pair + 16)
                    if end:
                        pe.wait_ge(out_lo, P - 1 + ONE)
                    else:
                        pe.wait_ge(out_summed, P + ONE)
                    bank = turned_bank(a, end)
                    for d in range(DC):
                        mm = pe.transpose(bank[:, d * 128:(d + 1) * 128], att_t[:, a, d * 128:(d + 1) * 128], f_ident)
                    mm.then_inc(out_turned, 1)
                else:
                    if k == 1 and piece != 1:
                        pe.wait_ge(out_lo, P + 1 + ONE)
                        if end:
                            pe.wait_ge(out_summed, P - 1 + ONE)
                    mm = split_product(projected_bank(a, end), turned_rows(a, end), wp_s[:], [6 * (k - 1) + p for p in passes])
                    if k == 2 and piece != 0:
                        mm.then_inc(out_projected, 1)

            def a_item(g, s, item, m, parity):
                v = 4 * g + s
                need(pe, a_used, m - 1)
                if item == 16:
                    pe.wait_ge(max_chain, 4 * v + 3)
                    pe.transpose(ps_a[0:16, parity, 0:128], max_parts[:, s % 2, :].bitcast(F32), f_ident).then_inc(a_ready, 1)
                    return
                t, half = item // 2, item % 2
                if item == 0:
                    pe.wait_ge(qk_in[s], 96 * g + 96)
                pe.matmul(ps_a[:, parity, :], q_stack[0:96, s, t * 128:(t + 1) * 128],
                          k_stack[0:96, s, half * 512:(half + 1) * 512], start=True, stop=True).then_inc(a_ready, 1)

            def turned_scores(g, s, k):
                if k == 0:
                    pe.wait_ge(row_in[s % 2], 64 * g + 32 * (s // 2) + 32)
                    if isinstance(g, int) and (g, s) == (0, 0):
                        pe.wait_ge(ones_set, 1)
                        pe.wait_ge(tile_ev, 8 * (LEAD - 1) + 6 + PAIR_BEFORE)
                need(pe, exp_done, 32 * g + 8 * s + k - 1)
                half, pair = k // 4, k % 4
                for e in range(2):
                    t = 2 * pair + e
                    mm = pe.matmul(ps_st[:, k % 2, e, :], k_stack[0:98, s, t * 128:(t + 1) * 128],
                                   q_stack[0:98, s, half * 512:(half + 1) * 512], start=True, stop=True)
                mm.then_inc(st_ready, 1)

            def sums(g, s, k):
                half, pair = k // 4, k % 4
                v = 4 * g + s
                if k == 0:
                    pe.wait_ge(v_in[s], 16 * g + 16)
                    if isinstance(g, int) and (g, s) == (0, 0):
                        pe.wait_ge(tile_ev, 8 * LEAD + PAIR_BEFORE)
                if pair == 0:
                    need(pe, o_chain, 3 * (2 * v + half - 1) + 2)
                pe.wait_ge(*low_count(g, 8 * s + k))
                for e in range(2):
                    for lo in range(2):
                        for t in range(4):
                            width = NL if lo else VP
                            tile = (p_lo if lo else p_hi)[:, k % 4, e * 512 + t * 128:e * 512 + (t + 1) * 128]
                            mm = pe.matmul(ps_o[:, t, 0:width], tile, v_head[:, s, 2 * pair + e, 0:width],
                                           start=(pair == 0 and e == 0 and lo == 0 and t == 0),
                                           stop=(pair == 3 and e == 1 and lo == 1 and t == 3), skip_group_check=True)
                mm.then_inc(pv_done, 1)

            pe.wait_ge(w_low, len(chunks) - NG)
            with pe.Fori(0, LEAD - 1) as p:
                for fill in range(8):
                    for part in range(1 if fill < 2 else 2):
                        stage(p, fill, part, lead=True)
            for step in range(LEAD_STEPS):
                for m in range(*LEAD_SPAN.get(step, (0, 0))):
                    v, item = lead_item(m)
                    a_item(0, v, item, m, m % 2)
                if step in LEAD_STAGE:
                    stage(LEAD - 1, *LEAD_STAGE[step], lead=True)
            turned_scores(0, 0, 0)

            def iteration(i, tiles, outs, first=False, last=False):
                pair = i - FIRST_OUTS
                for s in range(4):
                    for k in range(8):
                        step = 8 * s + k
                        uses = ring_uses(i, s, k, last)

                        def piece(at, n):
                            if tiles and at in PAIR_STAGE:
                                fill, part = PAIR_STAGE[at]
                                if fill == 0 and outs and n == 0:
                                    pe.wait_ge(out_summed, 2 * pair + ONE)
                                stage(i + LEAD, fill, part, piece=n)
                            if outs and at in OUT_STAGE:
                                a, part = OUT_STAGE[at]
                                if (a, part, n) == (0, 0, 0):
                                    pe.wait_ge(tile_ev, 8 * (i + LEAD + 1 if tiles else PAIRS) + PAIR_BEFORE)
                                out_part(pair, a, part, piece=n)

                        for use in uses[:1]:
                            a_item(*use)
                        if k < 7:
                            turned_scores(i, s, k + 1)
                        elif not (last and s == 3):
                            turned_scores(i + (s + 1) // 4, (s + 1) % 4, 0)
                        piece(step - 1, 1)
                        for use in uses[1:]:
                            a_item(*use)
                        if k >= SUM_LAG:
                            sums(i, s, k - SUM_LAG)
                        elif not (first and s == 0):
                            sums(i - (s == 0), (s - 1) % 4, k + 8 - SUM_LAG)
                        piece(step, 0)

            iteration(0, True, False, first=True)
            with pe.Fori(1, FIRST_OUTS) as i:
                iteration(i, True, False)
            with pe.Fori(FIRST_OUTS, LAST_TILES - 1) as i:
                iteration(i, True, True)
            iteration(LAST_TILES - 1, True, True)
            with pe.Fori(LAST_TILES, ITERS - 1) as i:
                iteration(i, False, True)
            iteration(ITERS - 1, False, True, last=True)
            for k in range(8 - SUM_LAG, 8):
                sums(ITERS - 1, 3, k)
            pe.wait_ge(exp_done, 8 * NV)
            with pe.Fori(ITERS - FIRST_OUTS, ITERS) as m:
                for a in range(2):
                    out_part(m, a, 0, end=True)
                for a in range(2):
                    for k in (1, 2):
                        out_part(m, a, k, end=True)

        @block.scalar
        def _(act):
            for c in range(len(chunks)):
                kind, w, part, _ = chunks[c]
                act.wait_ge(w_turned, c + 1)
                bank = ps_st[:, (c % 4) // 2, c % 2, :].rearrange("p (c n) -> p c n", c=DC)
                if kind == "g":
                    dst = modT[:, w * DC:(w + 1) * DC, part * 128:(part + 1) * 128]
                else:
                    dst = (wqkv_s[:, 0, w] if kind == "w" else wp_s[:, 0])[:, :, part * 128:(part + 1) * 128]
                nc.scalar.activation(dst, bank, ACT.Copy).then_inc(w_high, 1)
                if c == NG:
                    act.wait_ge(cond_turned, 1)
                    nc.scalar.activation(condT[:].rearrange("p c n -> p (c n)"), ps_w[:, 0:4 * DC], ACT.Copy
                                         ).then_inc(cond_ready, 1)

            act.wait_ge(s_bias, 64)

            def tile_high(pair, fill, lead=False):
                bank = bank_of(fill, lead)
                act.wait_ge(tile_mm, 8 * pair + fill + 1)
                if fill < 2:
                    nc.scalar.activation(hT_s[:, 0, :, fill * 128:(fill + 1) * 128],
                                         bank.rearrange("p (c n) -> p c n", c=DC), ACT.Copy).then_inc(tile_hi, 1)
                    return
                w, half = (fill - 2) // 2, fill % 2
                act.wait_ge(qk_out[half], 64 * pair + (0 if lead else 32 * w) + ONE)
                for c in range(2):
                    high = nc.scalar.activation(qk_slot(fill, 0, lead)[:, c * 256:(c + 1) * 256], bank[:, c * 256:(c + 1) * 256],
                                                ACT.Identity, bias=bqk_s[:, 2 * half + c, w:w + 1])
                high.then_inc(tile_hi, 1)

            def out_high(P, a, end=False):
                act.wait_ge(out_turned, P + 1 + ONE)
                if end:
                    act.wait_ge(out_projected, P - 1)
                nc.scalar.activation(turned_rows(a, end)[:, 0], turned_bank(a, end).rearrange("p (c n) -> p c n", c=DC),
                                     ACT.Copy).then_inc(out_hi, 1)

            def exps(i, step, between):
                n, k = 32 * i + step, step % 8
                act.wait_ge(st_ready, n + 1)
                need(act, *low_count(i, step - 4))
                scores = ps_st[:, k % 2, :, :].rearrange("p a n -> p (a n)")
                nc.scalar.activation(p32[:, k % 4, :], scores, ACT.Exp, bias=PROB_LIFT)
                between()
                need(act, pv_done, n - 3)
                nc.scalar.activation(p_hi[:, k % 4, :], scores, ACT.Exp, bias=PROB_LIFT).then_inc(exp_done, 1)

            with act.Fori(0, LEAD - 1) as p:
                for fill in range(6):
                    tile_high(p, fill, lead=True)
            for fill in range(6):
                tile_high(LEAD - 1, fill, lead=True)

            def iteration(i, tiles, outs, first=False):
                P0 = 2 * (i - FIRST_OUTS)
                for step in range(32):
                    fill = evacuated(PAIR_STAGE, step)
                    ready = tiles and fill is not None

                    def turned_high():
                        if ready and fill < 2:
                            tile_high(i + LEAD, fill)
                        if outs and OUT_STAGE.get(step - 1, (0, 1))[1] == 0:
                            a = OUT_STAGE[step - 1][0]
                            out_high(P0 + a, a)
                    if first and step == 2:
                        for half in range(2):
                            act.wait_ge(qk_out[half], 64 * LEAD + ONE)
                    exps(i, step, turned_high)
                    if ready and 2 <= fill < 6:
                        tile_high(i + LEAD, fill)

            iteration(0, True, False, first=True)
            with act.Fori(1, FIRST_OUTS) as i:
                iteration(i, True, False)
            with act.Fori(FIRST_OUTS, LAST_TILES - 1) as i:
                iteration(i, True, True)
            iteration(LAST_TILES - 1, True, True)
            with act.Fori(LAST_TILES, ITERS - 1) as i:
                iteration(i, False, True)
            iteration(ITERS - 1, False, True)
            with act.Fori(ITERS - FIRST_OUTS, ITERS) as m:
                for a in range(2):
                    out_high(2 * m + a, a, end=True)

        @block.vector
        def _(dve):
            V = nc.vector
            V.memset(v_parts[:, :, :, 0:1], 1.0)
            V.memset(k_stack[96:98, :, :].bitcast(F32), 1.0).then_inc(ones_set, 1)
            dve.wait_ge(s_bias, 64)
            for half in range(2):
                V.tensor_copy(bv_s[:, half * 256:(half + 1) * 256],
                              bias_stage[half].rearrange("p (d w) -> p d w", w=3)[:, :, 2]).then_inc(bv_ready, 1)

            dve.wait_ge(s_small, 80)
            for c in range(NG, len(chunks)):
                kind, w, part, _ = chunks[c]
                dve.wait_ge(w_high, c + 1)
                bank = ps_st[:, (c % 4) // 2, c % 2, :].rearrange("p (c n) -> p c n", c=DC)
                both = wqkv_s[:, :, w] if kind == "w" else wp_s[:]
                rows = slice(part * 128, (part + 1) * 128)
                V.tensor_tensor(both[:, 1, :, rows], bank, both[:, 0, :, rows].bitcast(F32), ALU.subtract
                                ).then_inc(w_low, 1)
                if c == NG + 5:
                    dve.wait_ge(mod_ready, 1)
                    V.tensor_tensor(small4[0], ps_a[0:4, 0, :], small4[3], ALU.add).then_inc(gain_chain, 1)
                    V.tensor_tensor(small4[4], ps_a[0:4, 1, :], small4[4], ALU.add).then_inc(gain_chain, 1)
                    dve.wait_ge(gain_chain, 2)
                    V.tensor_tensor(small4[3], small4[0], small4[1], ALU.mult).then_inc(gain_chain, 1)
                    V.tensor_tensor(small4[2], small4[0], small4[2], ALU.mult).then_inc(gain_chain, 1)
                    dve.wait_ge(gain_chain, 4)
                    V.tensor_tensor(small4[4], small4[4], small4[2], ALU.add).then_inc(gain_chain, 1)

            dve.wait_ge(bv_ready, 2)

            def stats(rows, bn, mv, done):
                V.bn_stats(bn, rows)
                dve.drain()
                V.bn_aggr(mv, bn).then_inc(done, 1)

            def tile_stats(pair, a):
                dve.wait_ge(x_in[a], 16 * pair + 16)
                need(dve, ln_pool, 8 * (pair - 1) + 4 * a + 4)
                stats(x_tile[:, a, :], bn_t[:, a, :], mv_t[:, a, :], ln_stat)

            def take(pair, fill, lead=False):
                bank = bank_of(fill, lead)
                if fill < 2:
                    dve.wait_ge(tile_hi, 6 * pair + fill + 1)
                    high, low = (hT_s[:, e, :, fill * 128:(fill + 1) * 128] for e in range(2))
                    V.tensor_tensor(low, bank.rearrange("p (c n) -> p c n", c=DC), high.bitcast(F32), ALU.subtract
                                    ).then_inc(tile_ev, 1)
                elif fill < 6:
                    w, half = (fill - 2) // 2, fill % 2
                    dve.wait_ge(tile_hi, 6 * pair + fill + 1)
                    for c in range(2):
                        cols = slice(c * 256, (c + 1) * 256)
                        rest = V.scalar_tensor_tensor(out=qk_slot(fill, 1, lead)[:, cols], in0=bank[:, cols],
                                                      scalar=bqk_s[:, 2 * half + c, w:w + 1],
                                                      in1=qk_slot(fill, 0, lead)[:, cols].bitcast(F32),
                                                      op0=ALU.add, op1=ALU.subtract)
                    rest.then_inc(tile_ev, 1)
                else:
                    a = fill - 6
                    dve.wait_ge(tile_mm, 8 * pair + fill + 1)
                    dve.wait_ge(v_pool, 4 * pair + ONE)
                    V.tensor_tensor(v_rest[:, a, :], bank, bv_s[:], ALU.add).then_inc(tile_ev, 1)
                    dve.wait_ge(tile_ev, 8 * pair + fill + 1 + PAIR_BEFORE)
                    dve.wait_ge(v_out[a], 16 * pair + ONE)
                    V.tensor_copy(v_parts[:, a, :, 1:1 + HD], v_rest[:, a, :].rearrange("p (h d) -> p h d", h=H)
                                  ).then_inc(v_dve, 1)

            def v_middle(pair, a):
                dve.wait_ge(v_pool, 4 * pair + 1 + a + ONE)
                V.tensor_copy(v_parts[:, a, :, 1 + HD:1 + 2 * HD], v_rest[:, a, :].rearrange("p (h d) -> p h d", h=H)
                              ).then_inc(v_dve, 1)

            def out_low(P, a, end=False):
                dve.wait_ge(out_hi, P + 1)
                high, low_part = (turned_rows(a, end)[:, e] for e in range(2))
                V.tensor_tensor(low_part, turned_bank(a, end).rearrange("p (c n) -> p c n", c=DC), high.bitcast(F32),
                                ALU.subtract).then_inc(out_lo, 1)

            def out_sum(pair, a, end=False):
                P = 2 * pair + a
                dve.wait_ge(out_projected, P + 1)
                dve.wait_ge(res_ready, P + 1)
                done = 5 * (pair + ITERS - FIRST_OUTS) if end else 10 * pair
                dve.wait_ge(out_pool, done + ONE)
                if end and a == 1:
                    dve.wait_ge(last_chain, 3 * (pair - (ITERS - FIRST_OUTS)) + ONE)
                V.tensor_tensor(h1_t[:, a, :], projected_bank(a, end), res_t[:, a, :], ALU.add).then_inc(out_summed, 1)

            def out_stats(P, a):
                dve.wait_ge(out_summed, P + 1 + ONE)
                stats(h1_t[:, a, :], obn_t[:, a, :], omv_t[:, a, :], out_stat)

            def last_norm(m):
                j = m - (ITERS - FIRST_OUTS)
                dve.wait_ge(last_std, j + 1)
                dve.wait_ge(last_out, 16 * j + ONE)
                dve.wait_ge(go_in, 16 * (ITERS - FIRST_OUTS) + 16)
                dve.wait_ge(y_out[1], 16 * (ITERS - FIRST_OUTS) + 16)
                y = y_t[:, 1, :]
                V.scalar_tensor_tensor(out=y, in0=h1_t[:, 1, :], scalar=omv_t[:, 1, 0:1], in1=go_s[:, 0, :],
                                       op0=ALU.subtract, op1=ALU.mult).then_inc(last_chain, 1)
                dve.wait_ge(last_chain, 3 * j + 1 + ONE)
                V.scalar_tensor_tensor(out=y, in0=y, scalar=ostd_t[:, 1, 1:2], in1=go_s[:, 1, :],
                                       op0=ALU.mult, op1=ALU.add).then_inc(last_chain, 1)
                dve.wait_ge(last_chain, 3 * j + 2 + ONE)
                V.tensor_tensor(y, y, h1_t[:, 1, :], ALU.add).then_inc(last_chain, 1)

            def ring_item(s, item, m, parity):
                dve.wait_ge(a_ready, m + 1)
                V.tensor_reduce(half_max[:, s % 2, item:item + 1], ps_a[:, parity, :], AX.X, ALU.max).then_inc(a_used, 1)

            def ring_row(g, s, m, parity):
                dve.wait_ge(a_ready, m + 1)
                need(dve, row_in[s % 2], 64 * g + 32 * (s // 2))
                V.tensor_copy(max_rows[:, s % 2, :], ps_a[0:16, parity, 0:128]).then_inc(max_chain, 1)
                dve.wait_ge(max_chain, 16 * g + 4 * s + 4)
                dve.sem_inc(a_used, 1)

            def max_split(g, s, m_last):
                e = s % 2
                chain = 16 * g + 4 * s
                dve.wait_ge(a_used, m_last + 1)
                V.tensor_reduce(neg_max[:, e, :], half_max[:, e, :].rearrange("p (t h) -> p t h", h=2), AX.X, ALU.max,
                                negate=True).then_inc(max_chain, 1)
                dve.wait_ge(max_chain, chain + 1)
                V.tensor_copy(max_parts[:, e, 0:8], neg_max[:, e, :]).then_inc(max_chain, 1)
                dve.wait_ge(max_chain, chain + 2)
                V.tensor_tensor(max_parts[:, e, 8:16], neg_max[:, e, :], max_parts[:, e, 0:8].bitcast(F32), ALU.subtract
                                ).then_inc(max_chain, 1)

            def low(i, step):
                n, k = 32 * i + step, step % 8
                dve.wait_ge(exp_done, n + 1)
                need(dve, pv_done, n - 3)
                V.tensor_tensor(p_lo[:, k % 4, :], p32[:, k % 4, :], p_hi[:, k % 4, :], ALU.subtract).then_inc(low_dve, 1)

            def normalise(g, s, half):
                v = 4 * g + s
                chain = 3 * (2 * v + half)
                dve.wait_ge(pv_done, 8 * v + 4 * half + 4)
                V.tensor_reduce(o_sum[:], ps_o[:, :, 1:VP].rearrange("p t (c d) -> p t d c", c=3), AX.X, ALU.add
                                ).then_inc(o_chain, 1)
                V.reciprocal(o_rcp[:], ps_o[:, :, 0]).then_inc(o_chain, 1)
                dve.wait_ge(o_chain, chain + 2)
                need(dve, att_out[half], 16 * v)
                V.scalar_tensor_tensor(out=o_out[:, half, :, :], in0=o_sum[:], scalar=ATT_SCALE,
                                       in1=o_rcp[:].unsqueeze(2).to_broadcast([128, 4, HD]),
                                       op0=ALU.mult, op1=ALU.mult).then_inc(o_chain, 1)

            for a in range(2):
                tile_stats(0, a)
            with dve.Fori(0, LEAD - 1) as p:
                for fill in range(8):
                    take(p, fill, lead=True)
                    if fill in (1, 3):
                        tile_stats(p + 1, fill // 2)
                for a in range(2):
                    v_middle(p, a)
            for step in range(LEAD_STEPS):
                for m in range(*LEAD_SPAN.get(step, (0, 0))):
                    v, item = lead_item(m)
                    if item == 16:
                        ring_row(0, v, m, m % 2)
                    else:
                        ring_item(v, item, m, m % 2)
                    if (v, item) == (0, 15):
                        max_split(0, 0, m)
                fill = evacuated(LEAD_STAGE, step)
                if fill is not None:
                    take(LEAD - 1, fill, lead=True)
                if step in (2, 5):
                    tile_stats(LEAD, step // 3)
            for a in range(2):
                v_middle(LEAD - 1, a)

            def iteration(i, tiles, norms, outs, first=False, last=False):
                pair = i - FIRST_OUTS
                for s in range(4):
                    for k in range(8):
                        step = 8 * s + k
                        uses = ring_uses(i, s, k, last)

                        def ring(some):
                            for g, sa, item, m, parity in some:
                                if item == 16:
                                    ring_row(g, sa, m, parity)
                                else:
                                    ring_item(sa, item, m, parity)
                                if item == 15:
                                    max_split(g, sa, m)
                        if k == 3 and not (first and s == 0):
                            normalise(i - (s == 0), (s - 1) % 4, 1)
                        if k == 7:
                            normalise(i, s, 0)
                        ring(uses[:1])
                        if tiles and evacuated(PAIR_STAGE, step - 1) in (2, 3, 4, 5):
                            take(i + LEAD, evacuated(PAIR_STAGE, step - 1))
                        before = (step - 2) % 32
                        if before not in POOL_LOW | DVE_LOW_EARLY and not (first and step == 0):
                            low(i - (step < 2), before)
                        ring(uses[1:])
                        if step - 1 in DVE_LOW_EARLY:
                            low(i, step - 1)
                        fill = evacuated(PAIR_STAGE, step)
                        if tiles and fill in (0, 1, 6, 7):
                            take(i + LEAD, fill)
                        if outs and step - 1 in OUT_STAGE:
                            a, part = OUT_STAGE[step - 1]
                            if part == 0:
                                out_low(2 * pair + a, a)
                            if part == 2:
                                out_sum(pair, a)
                        if norms and step in LN_STEP:
                            tile_stats(i + LEAD + 1, LN_STEP[step])
                        if tiles and step in V_MIDDLE_STEP:
                            v_middle(i + LEAD, V_MIDDLE_STEP[step])
                        if outs and step in OUT_STATS_STEP:
                            a = OUT_STATS_STEP[step]
                            out_stats(2 * pair + a, a)

            iteration(0, True, True, False, first=True)
            with dve.Fori(1, FIRST_OUTS) as i:
                iteration(i, True, True, False)
            with dve.Fori(FIRST_OUTS, LAST_TILES - 1) as i:
                iteration(i, True, True, True)
            iteration(LAST_TILES - 1, True, False, True)
            with dve.Fori(LAST_TILES, ITERS - 1) as i:
                iteration(i, False, False, True)
            iteration(ITERS - 1, False, False, True, last=True)
            low(ITERS - 1, 30)
            normalise(ITERS - 1, 3, 1)
            with dve.Fori(ITERS - FIRST_OUTS, ITERS) as m:
                for a in range(2):
                    out_low(2 * m + a, a, end=True)
                for a in (0, 1):
                    out_sum(m, a, end=True)
                    out_stats(2 * m + a, a)
                last_norm(m)

        @block.gpsimd
        def _(pool):
            G = nc.gpsimd
            for semaphore in start_at_one:
                pool.sem_inc(semaphore, ONE)
            pool.sem_inc(tile_ev, PAIR_BEFORE)
            G.memset(minus_half[:], -0.5)
            G.memset(eps_s[:], EPS)
            G.memset(zero_s[:], 0.0)
            G.memset(ident[:], 0.0).then_inc(id_zero, 1)
            pool.wait_ge(id_zero, 1)
            G.affine_select(out=ident[:], in_=ident[:], compare_op=ALU.not_equal, fill=1.0, base=0,
                            pattern=[[-1, 128]], channel_multiplier=1).then_inc(id_ready, 1)
            pool.wait_ge(id_ready, 1)
            for a in range(2):
                G.dma_start(mark_d[a], ident[0:1, 0:16]).then_inc(y_out[a], 16)

            def power(mv, std, chain):
                G.tensor_tensor(std[:, 1:2], mv[:, 1:2], eps_s[:], ALU.add)
                G.tensor_tensor(std[:, 0:1], zero_s[:], mv[:, 0:1], ALU.subtract)
                pool.drain()
                G.tensor_tensor(std[:, 1:2], std[:, 1:2], minus_half[:], ALU.pow).then_inc(chain, 1)
                pool.drain()

            def norm_scale(pair, a):
                pool.wait_ge(ln_stat, 2 * pair + a + 1)
                need(pool, tile_mm, 8 * (pair - 1) + a + 1)
                power(mv_t[:, a, :], std_t[:, a, :], ln_pool)
                G.tensor_scalar(h_tile[:, a, :], x_tile[:, a, :], std_t[:, a, 0:1], std_t[:, a, 1:2], ALU.add, ALU.mult
                                ).then_inc(ln_pool, 1)

            def norm_gain(pair, a):
                h = h_tile[:, a, :]
                pool.wait_ge(ln_pool, 8 * pair + 4 * a + 2)
                pool.wait_ge(gq_in, 16 * pair + 16)
                G.tensor_tensor(h, h, gq_s[:, 0, :], ALU.mult).then_inc(ln_pool, 1)
                pool.wait_ge(ln_pool, 8 * pair + 4 * a + 3)
                G.tensor_tensor(h, h, gq_s[:, 1, :], ALU.add).then_inc(ln_pool, 1)

            def v_take_high(pair, a):
                pool.wait_ge(v_dve, 4 * pair + 1 + a)
                rest = v_rest[:, a, :].rearrange("p (h d) -> p h d", h=H)
                G.tensor_tensor(rest, rest, v_parts[:, a, :, 1:1 + HD], ALU.subtract).then_inc(v_pool, 1)

            def v_take_middle(pair, a):
                pool.wait_ge(v_dve, 4 * pair + 3 + a)
                rest = v_rest[:, a, :].rearrange("p (h d) -> p h d", h=H)
                G.tensor_tensor(v_parts[:, a, :, 1 + 2 * HD:VP], rest, v_parts[:, a, :, 1 + HD:1 + 2 * HD], ALU.subtract
                                ).then_inc(v_pool, 1)

            def residual(pair, a):
                pool.wait_ge(res_in[a], 16 * pair + 16)
                G.tensor_tensor(res_t[:, a, :], res_t[:, a, :], bp_s[:], ALU.add).then_inc(res_ready, 1)

            def out_scale(pair, a, count, gains=None):
                pool.wait_ge(out_stat, 2 * pair + a + 1)
                pool.wait_ge(y_out[a], 16 * pair + 16)
                power(omv_t[:, a, :], ostd_t[:, a, :], out_pool)
                y = y_t[:, a, :]
                G.tensor_scalar(y, h1_t[:, a, :], ostd_t[:, a, 0:1], ostd_t[:, a, 1:2], ALU.add, ALU.mult
                                ).then_inc(out_pool, 1)
                pool.wait_ge(out_pool, count + 2)
                pool.wait_ge(go_in, 16 * pair + 16 if gains is None else gains)
                G.tensor_tensor(y, y, go_s[:, 0, :], ALU.mult).then_inc(out_pool, 1)

            def out_finish(pair, a, count):
                y = y_t[:, a, :]
                pool.wait_ge(out_pool, count + 3)
                G.tensor_tensor(y, y, go_s[:, 1, :], ALU.add).then_inc(out_pool, 1)
                pool.wait_ge(out_pool, count + 4)
                G.tensor_tensor(y, y, h1_t[:, a, :], ALU.add).then_inc(out_pool, 1)
                pool.wait_ge(out_pool, count + 5)
                G.dma_start(out_rows[bass.ds((2 * pair + a) * 128, 128), :], y).then_inc(y_out[a], 16)

            def end_pair(m):
                count = 5 * (m + ITERS - FIRST_OUTS) + ONE
                out_scale(m, 0, count, gains=16 * (ITERS - FIRST_OUTS) + 16)
                pool.wait_ge(out_stat, 2 * m + 2)
                pool.wait_ge(last_chain, 3 * (m - (ITERS - FIRST_OUTS)) + ONE)
                power(omv_t[:, 1, :], ostd_t[:, 1, :], last_std)
                out_finish(m, 0, count)

            def low(i, step):
                n, k = 32 * i + step, step % 8
                pool.wait_ge(exp_done, n + 1)
                need(pool, pv_done, n - 3)
                G.tensor_tensor(p_lo[:, k % 4, :], p32[:, k % 4, :], p_hi[:, k % 4, :], ALU.subtract).then_inc(low_pool, 1)

            def norm(pair, a):
                norm_scale(pair, a)
                norm_gain(pair, a)

            def v_rests(pair):
                for a in range(2):
                    v_take_high(pair, a)
                for a in range(2):
                    v_take_middle(pair, a)

            pool.wait_ge(bv_ready, 2)
            for a in range(2):
                norm(0, a)
            with pool.Fori(0, LEAD - 1) as p:
                for a in range(2):
                    norm(p + 1, a)
                v_rests(p)
            for a in range(2):
                norm(LEAD, a)
            v_rests(LEAD - 1)

            def iteration(i, tiles, norms, outs):
                pair = i - FIRST_OUTS
                ahead = i + LEAD
                for step in range(32):
                    if step in POOL_LOW:
                        low(i, step)
                    if norms and step in (7, 15):
                        norm_scale(ahead + 1, step // 8)
                    if norms and step in (9, 17):
                        norm_gain(ahead + 1, step // 8 - 1)
                    if tiles and step in (19, 21):
                        v_take_high(ahead, step // 2 - 9)
                    if tiles and step in (21, 23):
                        v_take_middle(ahead, step // 2 - 10)
                    if outs and step in (11, 13):
                        residual(pair, step // 2 - 5)
                    if outs and step in (27, 31):
                        a = step // 4 - 6
                        out_scale(pair, a, 10 * pair + 5 * a + ONE)
                    if outs and step in (29, 31):
                        a = step // 2 - 14
                        out_finish(pair, a, 10 * pair + 5 * a + ONE)

            iteration(0, True, True, False)
            with pool.Fori(1, FIRST_OUTS) as i:
                iteration(i, True, True, False)
            with pool.Fori(FIRST_OUTS, LAST_TILES - 1) as i:
                iteration(i, True, True, True)
            iteration(LAST_TILES - 1, True, False, True)
            with pool.Fori(LAST_TILES, ITERS - 1) as i:
                iteration(i, False, False, True)
            iteration(ITERS - 1, False, False, True)
            END = ITERS - FIRST_OUTS
            for a in range(2):
                residual(END, a)
            with pool.Fori(END, ITERS - 1) as m:
                end_pair(m)
                for a in range(2):
                    residual(m + 1, a)
            end_pair(ITERS - 1)


NAMES = ["x", "cond_1024"] + ["L0_cond_" + n for n in (
    "ln_g", "ln_b", "Wg", "bg", "Wb", "bb", "Wqkv", "bqkv", "Wp", "bp")]


def kernel(**inputs):
    import numpy as np
    import concourse.bacc as bacc
    from concourse.bass_utils import run_bass_kernel_spmd

    nc = bacc.Bacc("TRN2", target_bir_lowering=False, num_devices=1)
    arrays, args = {}, []
    for name in NAMES:
        a = np.ascontiguousarray(inputs[name])
        arrays[f"in_{name}"] = a
        args.append(nc.dram_tensor(f"in_{name}", a.shape, mybir.dt.from_np(a.dtype), kind="ExternalInput").ap())
    out = nc.dram_tensor("out_y", inputs["x"].shape, F32, kind="ExternalOutput").ap()
    conditioned_attention(nc, *args, out)
    result = run_bass_kernel_spmd(nc, [arrays], core_ids=[0])
    return result.results[0]["out_y"]
```

```python
from contextlib import ExitStack

import concourse.bass as bass
from concourse import mybir

ALU = mybir.AluOpType
ACT = mybir.ActivationFunctionType
AX = mybir.AxisListType
F32 = mybir.dt.float32
FR = mybir.dt.float32r
F16 = mybir.dt.float16
BF16 = mybir.dt.bfloat16

EPS = 1e-05
PROB_LIFT = 8.0

SPLIT = [(0, 0), (0, 1), (1, 0)]

PAIR_STAGE = {0: (0, 0), 2: (1, 0), 4: (2, 0), 5: (2, 1), 7: (3, 0), 8: (3, 1), 10: (4, 0), 11: (4, 1),
              13: (5, 0), 14: (5, 1), 16: (6, 0), 17: (6, 1), 19: (7, 0), 20: (7, 1)}
OUT_STAGE = {22: (0, 0), 24: (0, 1), 25: (0, 2), 27: (1, 0), 29: (1, 1), 30: (1, 2)}
PIECES = (range(0, 2), range(2, 6))
LN_STEP = {5: 0, 13: 1}
V_MIDDLE_STEP = {23: 0, 24: 1}
OUT_STATS_STEP = {27: 0, 31: 1}
NORM_SCALE_STEP = {7: 0, 15: 1}
NORM_GAIN_STEP = {9: 0, 17: 1}
RESIDUAL_STEP = {9: 0, 13: 1}
V_HIGH_STEP = {19: 0, 21: 1}
V_LOW_STEP = {21: 0, 23: 1}
OUT_SCALE_STEP = {27: 0, 31: 1}
OUT_FINISH_STEP = {29: 0, 31: 1}
V_STORE_STEP = {24: 0, 26: 1}
OUT_LOAD_STEP = 8
POOL_LOW = {4, 8, 12, 16, 20, 26} | set(range(1, 32, 2))
DVE_LOW_EARLY = {0, 24}
SUM_LAG = 3


def conditioned_attention(nc, x, cond, ln_g, ln_b, Wg, bg, Wb, bb, Wqkv, bqkv, Wp, bp, out):
    B, N, D = x.shape
    HD = 32
    H = D // HD
    DC = D // 128
    NV = B * H
    NT = B * N // 128
    ITERS = NV // 4
    PAIRS = NT // 2
    LEAD = N // 256 + 1
    VP = 3 * HD + 1
    NL = 2 * HD + 1
    ATT_SCALE = float(D) ** -0.5
    LAST_TILES = PAIRS - LEAD
    FIRST_OUTS = H // 4
    END = ITERS - FIRST_OUTS

    x_rows = x.rearrange("b n d -> (b n) d")
    out_rows = out.rearrange("b n d -> (b n) d")
    qk_d = nc.dram_tensor("qk_scratch", [4, B, D, N], F32, kind="Internal").ap()
    v_d = nc.dram_tensor("v_scratch", [NV, 128, N // 128, VP], BF16, kind="Internal").ap()
    att_d = nc.dram_tensor("att_scratch", [B * N, D], F32, kind="Internal").ap()
    gb_d = nc.dram_tensor("gain_bias_scratch", [PAIRS, 2, D], F32, kind="Internal").ap()
    mark_d = nc.dram_tensor("mark_scratch", [2, 1, 16], F32, kind="Internal").ap()
    att_heads = att_d.rearrange("(b e t p) (h d) -> b h e p t d", b=B, e=2, p=128, d=HD)
    qk_heads = qk_d.rearrange("w b (h d) n -> w (b h) d n", d=HD)
    qk_pairs = qk_d.rearrange("w b (c p) (t n) -> w b t p c n", p=128, n=256)
    v_tiles = v_d.rearrange("(b h) p t c -> b t p h c", b=B)

    with ExitStack() as ctx:
        def sb(name, shape, dt=F32):
            return ctx.enter_context(nc.sbuf_tensor(name, shape, dt))

        def sem(name):
            return ctx.enter_context(nc.semaphore(name))

        ps_st = ctx.enter_context(nc.psum_tensor("ps_st", [128, 2, 2, 512], F32))
        ps_a = ctx.enter_context(nc.psum_tensor("ps_a", [128, 2, 512], F32))
        ps_o = ctx.enter_context(nc.psum_tensor("ps_o", [128, 4, 128], F32))
        ps_w = ctx.enter_context(nc.psum_tensor("ps_w", [128, 512], F32))

        ident = sb("ident", [128, 128])
        wqkv_s = sb("wqkv_s", [128, 2, 3, DC, 512], FR)
        wp_s = sb("wp_s", [128, 2, DC, 512], FR)
        zero_s = sb("zero_s", [128, 1])
        eps_s = sb("eps_s", [128, 1])
        minus_half = sb("minus_half", [128, 1])
        bqk_s = sb("bqk_s", [128, DC, 3])
        bv_s = sb("bv_s", [128, D])
        bp_s = sb("bp_s", [128, D])
        gq_s = sb("gq_s", [128, 2, D])
        go_s = sb("go_s", [128, 2, D])
        q_stack = sb("q_stack", [128, 4, N], FR)
        k_stack = sb("k_stack", [128, 4, N], FR)
        v_head = sb("v_head", [128, 4, N // 128, VP], BF16)
        p32 = sb("p32", [128, 4, 1024])
        p_hi = sb("p_hi", [128, 4, 1024], F16)
        p_lo = sb("p_lo", [128, 4, 1024], F16)
        half_max = sb("half_max", [128, 2, 16])
        neg_max = sb("neg_max", [128, 2, 8])
        max_parts = sb("max_parts", [128, 2, 16], FR)
        max_rows = sb("max_rows", [16, 2, 128], FR)
        o_sum = sb("o_sum", [128, 4, HD])
        o_rcp = sb("o_rcp", [128, 4])
        o_out = sb("o_out", [128, 2, 4, HD])
        x_tile = sb("x_tile", [128, 2, D])
        h_tile = sb("h_tile", [128, 2, D])
        bn_t = sb("bn_t", [128, 2, 6])
        mv_t = sb("mv_t", [128, 2, 2])
        std_t = sb("std_t", [128, 2, 2])
        hT_s = sb("hT_s", [128, 2, DC, 256], FR)
        qkT_s = sb("qkT_s", [128, 2, 2, 512], FR)
        v_rest = sb("v_rest", [128, 2, 512])
        v_parts = sb("v_parts", [128, 2, H, VP], BF16)
        att_t = sb("att_t", [128, 2, D])
        res_t = sb("res_t", [128, 2, D])
        oT_s = sb("oT_s", [128, 2, DC, 128], FR)
        h1_t = sb("h1_t", [128, 2, D])
        y_t = sb("y_t", [128, 2, D])
        obn_t = sb("obn_t", [128, 2, 6])
        omv_t = sb("omv_t", [128, 2, 2])
        ostd_t = sb("ostd_t", [128, 2, 2])
        small4 = [att_t[0:4, 0, :], att_t[0:4, 1, :], h1_t[0:4, 0, :], res_t[0:4, 0, :], res_t[0:4, 1, :]]
        condT = sb("condT", [128, DC, 4])

        id_ready = sem("id_ready")
        ones_set = sem("ones_set")
        id_zero = sem("id_zero")
        s_small = sem("s_small")
        s_bias = sem("s_bias")
        bv_ready = sem("bv_ready")
        raw_in = [sem(f"raw_in{r}") for r in range(8)]
        w_turned = sem("w_turned")
        w_high = sem("w_high")
        w_low = sem("w_low")
        cond_turned = sem("cond_turned")
        cond_ready = sem("cond_ready")
        mod_ready = sem("mod_ready")
        gain_chain = sem("gain_chain")
        gain_stored = sem("gain_stored")
        qk_in = [sem(f"qk_in{s}") for s in range(4)]
        v_in = [sem(f"v_in{s}") for s in range(4)]
        row_in = [sem(f"row_in{s}") for s in range(2)]
        a_ready = sem("a_ready")
        a_used = sem("a_used")
        max_chain = sem("max_chain")
        st_ready = sem("st_ready")
        exp_done = sem("exp_done")
        low_dve = sem("low_dve")
        low_pool = sem("low_pool")
        pv_done = sem("pv_done")
        o_chain = sem("o_chain")
        att_out = [sem(f"att_out{s}") for s in range(2)]
        x_in = [sem(f"x_in{s}") for s in range(2)]
        gq_in = sem("gq_in")
        ln_stat = sem("ln_stat")
        ln_pool = sem("ln_pool")
        tile_mm = sem("tile_mm")
        tile_hi = sem("tile_hi")
        tile_ev = sem("tile_ev")
        v_dve = sem("v_dve")
        v_pool = sem("v_pool")
        qk_out = [sem(f"qk_out{s}") for s in range(2)]
        v_out = [sem(f"v_out{a}") for a in range(2)]
        att_in = [sem(f"att_in{s}") for s in range(2)]
        res_in = [sem(f"res_in{s}") for s in range(2)]
        go_in = sem("go_in")
        res_ready = sem("res_ready")
        out_turned = sem("out_turned")
        out_hi = sem("out_hi")
        out_lo = sem("out_lo")
        out_projected = sem("out_projected")
        out_summed = sem("out_summed")
        out_stat = sem("out_stat")
        out_pool = sem("out_pool")
        y_out = [sem(f"y_out{s}") for s in range(2)]
        last_std = sem("last_std")
        last_chain = sem("last_chain")
        last_out = sem("last_out")
        ONE = 1
        start_at_one = [*qk_out, *v_out, v_pool, out_turned, out_lo, out_summed, out_pool, last_chain, last_out]
        PAIR_BEFORE = 8

        def need(eng, semaphore, value):
            if not isinstance(value, int) or value > 0:
                eng.wait_ge(semaphore, value)

        wqkv_rows = Wqkv.rearrange("(j c) d -> c j d", c=3)
        chunks = [("g", 0, c, Wg[c * 128:(c + 1) * 128, :]) for c in range(DC)]
        chunks += [("g", 1, c, Wb[c * 128:(c + 1) * 128, :]) for c in range(DC)]
        chunks += [("w", w, c, wqkv_rows[w, c * 128:(c + 1) * 128, :]) for w in range(3) for c in range(DC)]
        chunks += [("p", 0, c, Wp[c * 128:(c + 1) * 128, :]) for c in range(DC)]
        NG = 2 * DC
        raw_slot = [half[:].rearrange("p a n -> p (a n)").bitcast(F32)[:, r * 512:(r + 1) * 512]
                    for half in (p_hi, p_lo) for r in range(4)]
        bias_stage = [buf[:].rearrange("p a d -> p (a d)")[:, 0:3 * D // 2] for buf in (h_tile, v_rest)]
        modT = p32[:].rearrange("p a (b n) -> p (a b) n", n=512)

        A_LEAD = 16 + 8 + 1

        def lead_item(k):
            return ([(0, q) for q in range(16)] + [(1, q) for q in range(4)] + [(0, 16)]
                    + [(1, q) for q in range(4, 8)])[k]

        LEAD_STAGE = dict(enumerate((f, part) for f in range(2, 8) for part in range(2)))
        LEAD_STEPS = 15
        LEAD_SPAN = {s + 2: (2 * s, 2 * s + 2) for s in range(9)} | {
            11: (18, 20), 12: (20, 21), 13: (21, 23), 14: (23, 25)}

        def ring_items(k):
            if k < 4:
                return [(2 * k, 1, 8 + 2 * k), (2 * k + 1, 1, 9 + 2 * k)]
            items = {4: [(8, 2, 0), (9, 2, 1)], 5: [(10, 1, 16), (11, 2, 2), (12, 2, 3)],
                     6: [(13, 2, 4), (14, 2, 5)], 7: [(15, 2, 6), (16, 2, 7)]}
            return items[k]

        def ring_uses(i, s, k, last):
            uses = []
            for pos, ahead, item in ring_items(k):
                if last and s + ahead > 3:
                    continue
                gone = 2 if last and s == 2 and item == 16 else 0
                uses.append((i + (s + ahead) // 4, (s + ahead) % 4, item,
                             A_LEAD + 17 * (4 * i + s) + pos - gone, (A_LEAD + 17 * s + pos) % 2))
            return uses

        pool_lows = sum(step in POOL_LOW for step in range(32))

        def low_count(i, step):
            i, step = i + step // 32, step % 32
            by_pool = step in POOL_LOW
            upto = sum((n in POOL_LOW) == by_pool for n in range(step + 1))
            return (low_pool, pool_lows * i + upto) if by_pool else (low_dve, (32 - pool_lows) * i + upto)

        def evacuated(stages, step):
            stage = stages.get(step - 1)
            return stage[0] if stage and (stage[1] == 1 or stage[0] < 2) else None

        LEAD_BANK = [ps_st[:, 0, 0, :], ps_st[:, 0, 1, :], ps_st[:, 1, 0, :], ps_st[:, 1, 1, :],
                     ps_st[:, 0, 0, :], ps_st[:, 0, 1, :], ps_w[:], ps_o[:].rearrange("p t c -> p (t c)")]
        LEAD_BEFORE = [4 - 8, 5 - 8, 2 - 8, 3 - 8, 0, 1, 6 - 8, 7 - 8]

        def bank_of(fill, lead):
            return LEAD_BANK[fill] if lead else ps_w[:]

        def qk_slot(fill, part, lead):
            if lead and fill > 3:
                return p32[:, fill - 2, part * 512:(part + 1) * 512].bitcast(FR)
            return qkT_s[:, fill % 2, part, :]

        def turned_bank(a, end):
            return ps_st[:, 0, a, :] if end else ps_w[:]

        def turned_rows(a, end):
            return hT_s[:, :, :, a * 128:(a + 1) * 128] if end else oT_s[:]

        def projected_bank(a, end):
            return ps_a[:, a, :] if end else ps_w[:]

        block = ctx.enter_context(nc.Block())

        @block.sync
        def _(sp):
            def load_gain(dst, dst_sem, pair):
                src = gb_d[bass.ds(pair, 1), :, :].rearrange("a c d -> a (c d)")
                sp.dma_start(dst[:].rearrange("p c d -> p (c d)"),
                             src.to_broadcast([128, 2 * D])).then_inc(dst_sem, 16)

            for r in range(8):
                sp.dma_start(raw_slot[r], chunks[r][3]).then_inc(raw_in[r], 16)
            sp.dma_start(small4[0], cond).then_inc(s_small, 16)
            for slot, row in ((1, ln_g), (2, ln_b), (3, bg), (4, bb)):
                sp.dma_start(small4[slot], row.rearrange("(a d) -> a d", a=1).to_broadcast([4, D])
                             ).then_inc(s_small, 16)
            sp.dma_start(bp_s[:], bp.rearrange("(a d) -> a d", a=1).to_broadcast([128, D])).then_inc(s_bias, 16)
            for half in range(2):
                sp.dma_start(bias_stage[half], bqkv.rearrange("(h d) -> h d", h=2)[half:half + 1].to_broadcast(
                    [128, 3 * D // 2])).then_inc(s_bias, 16)
            sp.dma_start(bqk_s[:], bqkv.rearrange("(c p w) -> p c w", p=128, w=3)).then_inc(s_bias, 16)
            for a in range(2):
                sp.dma_start(x_tile[:, a, :], x_rows[a * 128:(a + 1) * 128, :]).then_inc(x_in[a], 16)
            for c in range(8, len(chunks)):
                sp.wait_ge(w_turned, c - 7)
                sp.dma_start(raw_slot[c % 8], chunks[c][3]).then_inc(raw_in[c % 8], 16)
                if c == 17:
                    sp.wait_ge(gain_chain, 5)
                    batches = gb_d.rearrange("(b r) c d -> r b c d", b=B)
                    for r in range(PAIRS // B):
                        sp.dma_start(batches[r], res_t[0:4, :, :]).then_inc(gain_stored, 16)
                if c == 20:
                    sp.wait_ge(gain_stored, 16 * (PAIRS // B))
                    load_gain(gq_s, gq_in, 0)

            def at_tile(tiles, T):
                per = N // 128
                part = tiles[bass.ds(T // per, 1), bass.ds(T % per, 1)]
                return part.rearrange("b t p c n -> (b t p) c n")

            def load_x(pair, a):
                sp.dma_start(x_tile[:, a, :], x_rows[bass.ds((2 * pair + a) * 128, 128), :]).then_inc(x_in[a], 16)

            def store_rows(pair, fill, lead=False):
                w, half = (fill - 2) // 2, fill % 2
                per = N // 256
                sp.wait_ge(tile_ev, 8 * pair + fill + 1 + PAIR_BEFORE)
                for part in range(2):
                    dst = qk_pairs[2 * w + part, bass.ds(pair // per, 1), bass.ds(pair % per, 1), :, 2 * half:2 * half + 2, :]
                    sp.dma_start(dst.rearrange("b t p c n -> (b t p) c n"),
                                 qk_slot(fill, part, lead).bitcast(F32).rearrange("p (c n) -> p c n", n=256)
                                 ).then_inc(qk_out[half], 16)

            def store_v(pair, a):
                sp.wait_ge(v_pool, 4 * pair + 3 + a + ONE)
                sp.dma_start(at_tile(v_tiles, 2 * pair + a), v_parts[:, a]).then_inc(v_out[a], 16)

            def wait_pairs(pairs):
                for s in range(2):
                    sp.wait_ge(qk_out[s], 64 * pairs + ONE)
                    sp.wait_ge(v_out[s], 16 * pairs + ONE)

            def load_stacks(v, s):
                for row, part in ((0, 0), (1, 0), (2, 1)):
                    sp.dma_start(q_stack[row * HD:(row + 1) * HD, s, :].bitcast(F32),
                                 qk_heads[part, bass.ds(v, 1)].rearrange("a d n -> (a d) n")).then_inc(qk_in[s], 16)
                for row, part in ((0, 2), (1, 3), (2, 2)):
                    sp.dma_start(k_stack[row * HD:(row + 1) * HD, s, :].bitcast(F32),
                                 qk_heads[part, bass.ds(v, 1)].rearrange("a d n -> (a d) n")).then_inc(qk_in[s], 16)

            def load_v(v, s):
                sp.dma_start(v_head[:, s, :, :], v_d[bass.ds(v, 1)].rearrange("a p t c -> (a p) t c")
                             ).then_inc(v_in[s], 16)

            def store_row(v, s):
                sp.wait_ge(max_chain, 4 * v + 4)
                for part in range(2):
                    sp.dma_start(q_stack[96 + part:97 + part, s, :].bitcast(F32),
                                 max_rows[8 * part:8 * part + 8, s % 2, :].bitcast(F32)).then_inc(row_in[s % 2], 16)

            def store_att(v, half):
                sp.wait_ge(o_chain, 3 * (2 * v + half) + 3)
                sp.dma_start(att_heads[bass.ds(v // H, 1), bass.ds(v % H, 1), half].rearrange("b h p t d -> (b h p) t d"),
                             o_out[:, half, :, :]).then_inc(att_out[half], 16)

            def load_att(pair, a):
                sp.wait_ge(out_turned, 2 * pair + ONE)
                sp.dma_start(att_t[:, a, :], att_d[bass.ds((2 * pair + a) * 128, 128), :]).then_inc(att_in[a], 16)

            def load_residual(pair, a, end=False):
                sp.wait_ge(out_summed, 2 * pair + (a - 1 if end else 0) + ONE)
                sp.dma_start(res_t[:, a, :], x_rows[bass.ds((2 * pair + a) * 128, 128), :]).then_inc(res_in[a], 16)

            def store_last(m):
                sp.wait_ge(last_chain, 4 * (m - END) + 4 + ONE)
                sp.dma_start(out_rows[bass.ds((2 * m + 1) * 128, 128), :], y_t[:, 1, :]).then_inc(last_out, 16)

            sp.wait_ge(ln_pool, 8)
            load_gain(gq_s, gq_in, 1)
            for a in range(2):
                load_x(1, a)
            with sp.Fori(0, LEAD - 2) as p:
                for fill in range(2, 6):
                    store_rows(p, fill, lead=True)
                sp.wait_ge(ln_pool, 8 * p + 16)
                load_gain(gq_s, gq_in, p + 2)
                for a in range(2):
                    load_x(p + 2, a)
                for a in range(2):
                    store_v(p, a)
            for fill in range(2, 6):
                store_rows(LEAD - 2, fill, lead=True)
            for s in range(2):
                sp.wait_ge(qk_out[s], 64 * (LEAD - 1) + ONE)
            load_stacks(0, 0)
            load_stacks(1, 1)
            sp.wait_ge(ln_pool, 8 * LEAD)
            load_gain(gq_s, gq_in, LEAD)
            for a in range(2):
                load_x(LEAD, a)
            for a in range(2):
                store_v(LEAD - 2, a)
            load_stacks(2, 2)
            for a in range(2):
                sp.wait_ge(v_out[a], 16 * (LEAD - 1) + ONE)
            for v in range(3):
                load_v(v, v)
            for fill in range(2, 6):
                store_rows(LEAD - 1, fill, lead=True)
            store_row(0, 0)
            for a in range(2):
                store_v(LEAD - 1, a)

            def iteration(i, tiles, norms, outs, first=False, last=False):
                pair = i - FIRST_OUTS
                for s in range(4):
                    u = 4 * i + s
                    for k in range(8):
                        step = 8 * s + k
                        if step == 0:
                            if norms:
                                sp.wait_ge(ln_pool, 8 * (i + LEAD + 1))
                                load_gain(gq_s, gq_in, i + LEAD + 1)
                                for a in range(2):
                                    load_x(i + LEAD + 1, a)
                            wait_pairs(i + LEAD if tiles else PAIRS)
                        if k == 0 and not (first and s == 0):
                            store_att(u - 1, 0)
                        if k == 1 and not (last and s > 0):
                            need(sp, st_ready, 8 * u)
                            load_stacks(u + 3, (s + 3) % 4)
                        if k == 4 and not (first and s == 0):
                            store_att(u - 1, 1)
                        if k == 4 and not (last and s > 0):
                            need(sp, pv_done, 8 * u)
                            load_v(u + 3, (s + 3) % 4)
                        if k == 6 and not (last and s == 3):
                            store_row(u + 1, (s + 1) % 4)
                        if outs and step == OUT_LOAD_STEP:
                            sp.wait_ge(out_pool, 10 * pair + ONE)
                            load_gain(go_s, go_in, pair)
                            for half in range(2):
                                sp.wait_ge(att_out[half], 64 * i)
                            for a in range(2):
                                load_att(pair, a)
                                load_residual(pair, a)
                        if tiles:
                            for fill in range(2, 6):
                                if evacuated(PAIR_STAGE, step - 2) == fill:
                                    store_rows(i + LEAD, fill)
                            if step in V_STORE_STEP:
                                store_v(i + LEAD, V_STORE_STEP[step])

            iteration(0, True, True, False, first=True)
            with sp.Fori(1, FIRST_OUTS) as i:
                iteration(i, True, True, False)
            with sp.Fori(FIRST_OUTS, LAST_TILES - 1) as i:
                iteration(i, True, True, True)
            iteration(LAST_TILES - 1, True, False, True)
            with sp.Fori(LAST_TILES, ITERS - 1) as i:
                iteration(i, False, False, True)
            iteration(ITERS - 1, False, False, True, last=True)
            store_att(NV - 1, 0)
            for a in range(2):
                load_residual(END, a, end=True)
            store_att(NV - 1, 1)
            for half in range(2):
                sp.wait_ge(att_out[half], 16 * NV)
            for a in range(2):
                load_att(END, a)
            sp.wait_ge(out_pool, 10 * END + ONE)
            load_gain(go_s, go_in, END)
            with sp.Fori(END, ITERS - 1) as m:
                for a in range(2):
                    load_att(m + 1, a)
                for a in range(2):
                    load_residual(m + 1, a, end=True)
                store_last(m)
            store_last(ITERS - 1)
            for a in range(2):
                sp.wait_ge(y_out[a], 16 * (1 + PAIRS - a * FIRST_OUTS))
            sp.wait_ge(last_out, 16 * FIRST_OUTS + ONE)

        @block.tensor
        def _(pe):
            f_ident = ident[:]

            def split_product(dst, left, right, count=range(12)):
                for n in count:
                    c, (lp, rp) = n // 3, SPLIT[n % 3]
                    mm = pe.matmul(dst, left[:, lp, c, :], right[:, rp, c, :], start=(n == 0), stop=(n == 11))
                return mm

            pe.wait_ge(id_ready, 1)
            for c in range(len(chunks)):
                pe.wait_ge(raw_in[c % 8], 16 * (c // 8 + 1))
                if c >= 4:
                    if c - 4 < NG:
                        pe.wait_ge(w_high, c - 3)
                    else:
                        pe.wait_ge(w_low, c - 3 - NG)
                bank = ps_st[:, (c % 4) // 2, c % 2, :]
                for d in range(DC):
                    mm = pe.transpose(bank[:, d * 128:(d + 1) * 128], raw_slot[c % 8][:, d * 128:(d + 1) * 128], f_ident)
                mm.then_inc(w_turned, 1)
                if c == NG - 1:
                    pe.wait_ge(s_small, 80)
                    for d in range(DC):
                        mm = pe.transpose(ps_w[:, d * 4:d * 4 + 4], small4[0][:, d * 128:(d + 1) * 128], f_ident[0:4, 0:4])
                    mm.then_inc(cond_turned, 1)
                    pe.wait_ge(cond_ready, 1)
                    for m in range(2):
                        for d in range(DC):
                            mm = pe.matmul(ps_a[0:4, m, :], condT[:, d, :],
                                           modT[:, m * DC + d, :], start=(d == 0), stop=(d == DC - 1))
                    mm.then_inc(mod_ready, 1)

            def stage(pair, fill, part, lead=False, piece=None):
                bank = bank_of(fill, lead)
                if fill < 2 and piece == 1:
                    return
                passes = range(6) if piece is None else PIECES[piece]
                ends = piece != 0
                if part == 0 and piece != 1:
                    before = LEAD_BEFORE[fill] if lead else fill - 1
                    pe.wait_ge(tile_ev, 8 * pair + before + 1 + PAIR_BEFORE)
                if fill < 2:
                    pe.wait_ge(ln_pool, 8 * pair + 4 * fill + 4)
                    for d in range(DC):
                        mm = pe.transpose(bank[:, d * 128:(d + 1) * 128], h_tile[:, fill, d * 128:(d + 1) * 128], f_ident)
                    mm.then_inc(tile_mm, 1)
                    return
                if fill == 2 and part == 0 and piece != 1:
                    pe.wait_ge(tile_ev, 8 * pair + 2 + PAIR_BEFORE)
                if fill < 6:
                    w, chunk = (fill - 2) // 2, 2 * (fill % 2) + part
                    for n in [n for p in passes for n in (2 * p, 2 * p + 1)]:
                        d, (lp, rp) = n // 3, SPLIT[n % 3]
                        mm = pe.matmul(bank[:, part * 256:(part + 1) * 256],
                                       wqkv_s[:, lp, w, d, chunk * 128:(chunk + 1) * 128], hT_s[:, rp, d, :],
                                       start=(n == 0), stop=(n == 11))
                else:
                    tokens = slice((fill - 6) * 128, (fill - 5) * 128)
                    mm = split_product(bank, hT_s[:, :, :, tokens], wqkv_s[:, :, 2], [6 * part + p for p in passes])
                if part == 1 and ends:
                    mm.then_inc(tile_mm, 1)

            def out_part(pair, a, k, end=False, piece=None):
                P = 2 * pair + a
                if k == 0 and piece == 1:
                    return
                passes = range(6) if piece is None else PIECES[piece]
                if k == 0:
                    pe.wait_ge(att_in[a], 16 * pair + 16)
                    if end:
                        pe.wait_ge(out_lo, P - 1 + ONE)
                    else:
                        pe.wait_ge(out_summed, P + ONE)
                    bank = turned_bank(a, end)
                    for d in range(DC):
                        mm = pe.transpose(bank[:, d * 128:(d + 1) * 128], att_t[:, a, d * 128:(d + 1) * 128], f_ident)
                    mm.then_inc(out_turned, 1)
                else:
                    if k == 1 and piece != 1:
                        pe.wait_ge(out_lo, P + 1 + ONE)
                        if end:
                            pe.wait_ge(out_summed, P - 1 + ONE)
                    mm = split_product(projected_bank(a, end), turned_rows(a, end), wp_s[:], [6 * (k - 1) + p for p in passes])
                    if k == 2 and piece != 0:
                        mm.then_inc(out_projected, 1)

            def a_item(g, s, item, m, parity):
                v = 4 * g + s
                need(pe, a_used, m - 1)
                if item == 16:
                    pe.wait_ge(max_chain, 4 * v + 3)
                    pe.transpose(ps_a[0:16, parity, 0:128], max_parts[:, s % 2, :].bitcast(F32), f_ident).then_inc(a_ready, 1)
                    return
                t, half = item // 2, item % 2
                if item == 0:
                    pe.wait_ge(qk_in[s], 96 * g + 96)
                pe.matmul(ps_a[:, parity, :], q_stack[0:96, s, t * 128:(t + 1) * 128],
                          k_stack[0:96, s, half * 512:(half + 1) * 512], start=True, stop=True).then_inc(a_ready, 1)

            def turned_scores(g, s, k):
                if k == 0:
                    pe.wait_ge(row_in[s % 2], 64 * g + 32 * (s // 2) + 32)
                    if isinstance(g, int) and (g, s) == (0, 0):
                        pe.wait_ge(ones_set, 1)
                        pe.wait_ge(tile_ev, 8 * (LEAD - 1) + 6 + PAIR_BEFORE)
                need(pe, exp_done, 32 * g + 8 * s + k - 1)
                half, pair = k // 4, k % 4
                for e in range(2):
                    t = 2 * pair + e
                    mm = pe.matmul(ps_st[:, k % 2, e, :], k_stack[0:98, s, t * 128:(t + 1) * 128],
                                   q_stack[0:98, s, half * 512:(half + 1) * 512], start=True, stop=True)
                mm.then_inc(st_ready, 1)

            def sums(g, s, k):
                half, pair = k // 4, k % 4
                v = 4 * g + s
                if k == 0:
                    pe.wait_ge(v_in[s], 16 * g + 16)
                    if isinstance(g, int) and (g, s) == (0, 0):
                        pe.wait_ge(tile_ev, 8 * LEAD + PAIR_BEFORE)
                if pair == 0:
                    need(pe, o_chain, 3 * (2 * v + half - 1) + 2)
                pe.wait_ge(*low_count(g, 8 * s + k))
                for e in range(2):
                    for lo in range(2):
                        for t in range(4):
                            width = NL if lo else VP
                            tile = (p_lo if lo else p_hi)[:, k % 4, e * 512 + t * 128:e * 512 + (t + 1) * 128]
                            mm = pe.matmul(ps_o[:, t, 0:width], tile, v_head[:, s, 2 * pair + e, 0:width],
                                           start=(pair == 0 and e == 0 and lo == 0 and t == 0),
                                           stop=(pair == 3 and e == 1 and lo == 1 and t == 3), skip_group_check=True)
                mm.then_inc(pv_done, 1)

            pe.wait_ge(w_low, len(chunks) - NG)
            for a in range(2):
                stage(0, a, 0, lead=True)
            with pe.Fori(0, LEAD - 1) as p:
                for fill in range(2, 8):
                    for part in range(2):
                        stage(p, fill, part, lead=True)
                for a in range(2):
                    stage(p + 1, a, 0, lead=True)
            for step in range(LEAD_STEPS):
                for m in range(*LEAD_SPAN.get(step, (0, 0))):
                    v, item = lead_item(m)
                    a_item(0, v, item, m, m % 2)
                if step in LEAD_STAGE:
                    stage(LEAD - 1, *LEAD_STAGE[step], lead=True)
            turned_scores(0, 0, 0)

            def iteration(i, tiles, outs, first=False, last=False):
                pair = i - FIRST_OUTS
                for s in range(4):
                    for k in range(8):
                        step = 8 * s + k
                        uses = ring_uses(i, s, k, last)

                        def piece(at, n):
                            if tiles and at in PAIR_STAGE:
                                fill, part = PAIR_STAGE[at]
                                if fill == 0 and outs and n == 0:
                                    pe.wait_ge(out_summed, 2 * pair + ONE)
                                stage(i + LEAD, fill, part, piece=n)
                            if outs and at in OUT_STAGE:
                                a, part = OUT_STAGE[at]
                                if (a, part, n) == (0, 0, 0):
                                    pe.wait_ge(tile_ev, 8 * (i + LEAD + 1 if tiles else PAIRS) + PAIR_BEFORE)
                                out_part(pair, a, part, piece=n)

                        for use in uses[:1]:
                            a_item(*use)
                        if k < 7:
                            turned_scores(i, s, k + 1)
                        elif not (last and s == 3):
                            turned_scores(i + (s + 1) // 4, (s + 1) % 4, 0)
                        piece(step - 1, 1)
                        for use in uses[1:]:
                            a_item(*use)
                        if k >= SUM_LAG:
                            sums(i, s, k - SUM_LAG)
                        elif not (first and s == 0):
                            sums(i - (s == 0), (s - 1) % 4, k + 8 - SUM_LAG)
                        piece(step, 0)

            iteration(0, True, False, first=True)
            with pe.Fori(1, FIRST_OUTS) as i:
                iteration(i, True, False)
            with pe.Fori(FIRST_OUTS, LAST_TILES - 1) as i:
                iteration(i, True, True)
            iteration(LAST_TILES - 1, True, True)
            with pe.Fori(LAST_TILES, ITERS - 1) as i:
                iteration(i, False, True)
            iteration(ITERS - 1, False, True, last=True)
            for k in range(8 - SUM_LAG, 8):
                sums(ITERS - 1, 3, k)
            pe.wait_ge(exp_done, 8 * NV)
            for a in range(2):
                out_part(END, a, 0, end=True)
            with pe.Fori(END, ITERS - 1) as m:
                for a in range(2):
                    for k in (1, 2):
                        out_part(m, a, k, end=True)
                for a in range(2):
                    out_part(m + 1, a, 0, end=True)
            for a in range(2):
                for k in (1, 2):
                    out_part(ITERS - 1, a, k, end=True)

        @block.scalar
        def _(act):
            for c in range(len(chunks)):
                kind, w, part, _ = chunks[c]
                act.wait_ge(w_turned, c + 1)
                bank = ps_st[:, (c % 4) // 2, c % 2, :].rearrange("p (c n) -> p c n", c=DC)
                if kind == "g":
                    dst = modT[:, w * DC:(w + 1) * DC, part * 128:(part + 1) * 128]
                else:
                    dst = (wqkv_s[:, 0, w] if kind == "w" else wp_s[:, 0])[:, :, part * 128:(part + 1) * 128]
                nc.scalar.activation(dst, bank, ACT.Copy).then_inc(w_high, 1)
                if c == NG - 1:
                    act.wait_ge(cond_turned, 1)
                    nc.scalar.activation(condT[:].rearrange("p c n -> p (c n)"), ps_w[:, 0:4 * DC], ACT.Copy
                                         ).then_inc(cond_ready, 1)

            act.wait_ge(s_bias, 64)

            def tile_high(pair, fill, lead=False):
                bank = bank_of(fill, lead)
                act.wait_ge(tile_mm, 8 * pair + fill + 1)
                if fill < 2:
                    nc.scalar.activation(hT_s[:, 0, :, fill * 128:(fill + 1) * 128],
                                         bank.rearrange("p (c n) -> p c n", c=DC), ACT.Copy).then_inc(tile_hi, 1)
                    return
                w, half = (fill - 2) // 2, fill % 2
                act.wait_ge(qk_out[half], 64 * pair + (0 if lead else 32 * w) + ONE)
                for c in range(2):
                    high = nc.scalar.activation(qk_slot(fill, 0, lead)[:, c * 256:(c + 1) * 256], bank[:, c * 256:(c + 1) * 256],
                                                ACT.Identity, bias=bqk_s[:, 2 * half + c, w:w + 1])
                high.then_inc(tile_hi, 1)

            def out_high(P, a, end=False):
                act.wait_ge(out_turned, P + 1 + ONE)
                if end:
                    act.wait_ge(out_projected, P - 1)
                nc.scalar.activation(turned_rows(a, end)[:, 0], turned_bank(a, end).rearrange("p (c n) -> p c n", c=DC),
                                     ACT.Copy).then_inc(out_hi, 1)

            def exps(i, step, between):
                n, k = 32 * i + step, step % 8
                act.wait_ge(st_ready, n + 1)
                need(act, *low_count(i, step - 4))
                scores = ps_st[:, k % 2, :, :].rearrange("p a n -> p (a n)")
                nc.scalar.activation(p32[:, k % 4, :], scores, ACT.Exp, bias=PROB_LIFT)
                between()
                need(act, pv_done, n - 3)
                nc.scalar.activation(p_hi[:, k % 4, :], scores, ACT.Exp, bias=PROB_LIFT).then_inc(exp_done, 1)

            for a in range(2):
                tile_high(0, a, lead=True)
            with act.Fori(0, LEAD - 1) as p:
                for fill in range(2, 6):
                    tile_high(p, fill, lead=True)
                for a in range(2):
                    tile_high(p + 1, a, lead=True)
            for fill in range(2, 6):
                tile_high(LEAD - 1, fill, lead=True)

            def iteration(i, tiles, outs, first=False):
                P0 = 2 * (i - FIRST_OUTS)
                for step in range(32):
                    fill = evacuated(PAIR_STAGE, step)
                    ready = tiles and fill is not None

                    def turned_high():
                        if ready and fill < 2:
                            tile_high(i + LEAD, fill)
                        if outs and OUT_STAGE.get(step - 1, (0, 1))[1] == 0:
                            a = OUT_STAGE[step - 1][0]
                            out_high(P0 + a, a)
                    if first and step == 2:
                        for half in range(2):
                            act.wait_ge(qk_out[half], 64 * LEAD + ONE)
                    exps(i, step, turned_high)
                    if ready and 2 <= fill < 6:
                        tile_high(i + LEAD, fill)

            iteration(0, True, False, first=True)
            with act.Fori(1, FIRST_OUTS) as i:
                iteration(i, True, False)
            with act.Fori(FIRST_OUTS, LAST_TILES - 1) as i:
                iteration(i, True, True)
            iteration(LAST_TILES - 1, True, True)
            with act.Fori(LAST_TILES, ITERS - 1) as i:
                iteration(i, False, True)
            iteration(ITERS - 1, False, True)
            with act.Fori(END, ITERS) as m:
                for a in range(2):
                    out_high(2 * m + a, a, end=True)

        @block.vector
        def _(dve):
            V = nc.vector
            V.memset(v_parts[:, :, :, 0:1], 1.0)
            V.memset(k_stack[96:98, :, :].bitcast(F32), 1.0).then_inc(ones_set, 1)
            dve.wait_ge(s_bias, 64)
            for half in range(2):
                V.tensor_copy(bv_s[:, half * 256:(half + 1) * 256],
                              bias_stage[half].rearrange("p (d w) -> p d w", w=3)[:, :, 2]).then_inc(bv_ready, 1)

            def stats(rows, bn, mv, done):
                V.bn_stats(bn, rows)
                dve.drain()
                V.bn_aggr(mv, bn).then_inc(done, 1)

            def tile_stats(pair, a):
                dve.wait_ge(x_in[a], 16 * pair + 16)
                need(dve, ln_pool, 8 * (pair - 1) + 4 * a + 4)
                stats(x_tile[:, a, :], bn_t[:, a, :], mv_t[:, a, :], ln_stat)

            for a in range(2):
                tile_stats(0, a)

            dve.wait_ge(s_small, 80)
            dve.wait_ge(mod_ready, 1)
            V.tensor_tensor(small4[0], ps_a[0:4, 0, :], small4[3], ALU.add).then_inc(gain_chain, 1)
            V.tensor_tensor(small4[4], ps_a[0:4, 1, :], small4[4], ALU.add).then_inc(gain_chain, 1)
            dve.wait_ge(gain_chain, 2)
            V.tensor_tensor(small4[3], small4[0], small4[1], ALU.mult).then_inc(gain_chain, 1)
            V.tensor_tensor(small4[2], small4[0], small4[2], ALU.mult).then_inc(gain_chain, 1)
            dve.wait_ge(gain_chain, 4)
            V.tensor_tensor(small4[4], small4[4], small4[2], ALU.add).then_inc(gain_chain, 1)
            for c in range(NG, len(chunks)):
                kind, w, part, _ = chunks[c]
                dve.wait_ge(w_high, c + 1)
                bank = ps_st[:, (c % 4) // 2, c % 2, :].rearrange("p (c n) -> p c n", c=DC)
                both = wqkv_s[:, :, w] if kind == "w" else wp_s[:]
                rows = slice(part * 128, (part + 1) * 128)
                V.tensor_tensor(both[:, 1, :, rows], bank, both[:, 0, :, rows].bitcast(F32), ALU.subtract
                                ).then_inc(w_low, 1)
            dve.wait_ge(bv_ready, 2)

            def take(pair, fill, lead=False):
                bank = bank_of(fill, lead)
                if fill < 2:
                    dve.wait_ge(tile_hi, 6 * pair + fill + 1)
                    high, low = (hT_s[:, e, :, fill * 128:(fill + 1) * 128] for e in range(2))
                    V.tensor_tensor(low, bank.rearrange("p (c n) -> p c n", c=DC), high.bitcast(F32), ALU.subtract
                                    ).then_inc(tile_ev, 1)
                elif fill < 6:
                    w, half = (fill - 2) // 2, fill % 2
                    dve.wait_ge(tile_hi, 6 * pair + fill + 1)
                    for c in range(2):
                        cols = slice(c * 256, (c + 1) * 256)
                        rest = V.scalar_tensor_tensor(out=qk_slot(fill, 1, lead)[:, cols], in0=bank[:, cols],
                                                      scalar=bqk_s[:, 2 * half + c, w:w + 1],
                                                      in1=qk_slot(fill, 0, lead)[:, cols].bitcast(F32),
                                                      op0=ALU.add, op1=ALU.subtract)
                    rest.then_inc(tile_ev, 1)
                else:
                    a = fill - 6
                    dve.wait_ge(tile_mm, 8 * pair + fill + 1)
                    dve.wait_ge(v_pool, 4 * pair + ONE)
                    V.tensor_tensor(v_rest[:, a, :], bank, bv_s[:], ALU.add).then_inc(tile_ev, 1)

            def v_high(pair, a):
                dve.wait_ge(tile_ev, 8 * pair + 7 + a + PAIR_BEFORE)
                dve.wait_ge(v_out[a], 16 * pair + ONE)
                V.tensor_copy(v_parts[:, a, :, 1:1 + HD], v_rest[:, a, :].rearrange("p (h d) -> p h d", h=H)
                              ).then_inc(v_dve, 1)

            def v_middle(pair, a):
                dve.wait_ge(v_pool, 4 * pair + 1 + a + ONE)
                V.tensor_copy(v_parts[:, a, :, 1 + HD:1 + 2 * HD], v_rest[:, a, :].rearrange("p (h d) -> p h d", h=H)
                              ).then_inc(v_dve, 1)

            def out_low(P, a, end=False):
                dve.wait_ge(out_hi, P + 1)
                high, low_part = (turned_rows(a, end)[:, e] for e in range(2))
                V.tensor_tensor(low_part, turned_bank(a, end).rearrange("p (c n) -> p c n", c=DC), high.bitcast(F32),
                                ALU.subtract).then_inc(out_lo, 1)

            def out_sum(pair, a):
                P = 2 * pair + a
                dve.wait_ge(out_projected, P + 1)
                dve.wait_ge(res_ready, P + 1)
                dve.wait_ge(out_pool, 10 * pair + ONE)
                V.tensor_tensor(h1_t[:, a, :], ps_w[:], res_t[:, a, :], ALU.add).then_inc(out_summed, 1)

            def end_sum(m, a):
                dve.wait_ge(out_projected, 2 * m + a + 1)
                dve.wait_ge(out_pool, 5 * (m + END) + ONE)
                h1 = h1_t[:, a, :]
                if a == 0:
                    dve.wait_ge(res_ready, m + END + 1)
                    V.tensor_tensor(h1, projected_bank(a, True), res_t[:, a, :], ALU.add).then_inc(out_summed, 1)
                else:
                    dve.wait_ge(res_in[1], 16 * m + 16)
                    dve.wait_ge(last_chain, 4 * (m - END) + ONE)
                    V.tensor_tensor(h1, projected_bank(a, True), res_t[:, a, :], ALU.add).then_inc(last_chain, 1)
                    dve.wait_ge(last_chain, 4 * (m - END) + 1 + ONE)
                    V.tensor_tensor(h1, h1, bp_s[:], ALU.add).then_inc(out_summed, 1)

            def out_stats(P, a):
                dve.wait_ge(out_summed, P + 1 + ONE)
                stats(h1_t[:, a, :], obn_t[:, a, :], omv_t[:, a, :], out_stat)

            def last_norm(m):
                j = m - END
                dve.wait_ge(last_std, j + 1)
                dve.wait_ge(last_out, 16 * j + ONE)
                dve.wait_ge(go_in, 16 * END + 16)
                dve.wait_ge(y_out[1], 16 * END + 16)
                y = y_t[:, 1, :]
                V.scalar_tensor_tensor(out=y, in0=h1_t[:, 1, :], scalar=omv_t[:, 1, 0:1], in1=go_s[:, 0, :],
                                       op0=ALU.subtract, op1=ALU.mult).then_inc(last_chain, 1)
                dve.wait_ge(last_chain, 4 * j + 2 + ONE)
                V.scalar_tensor_tensor(out=y, in0=y, scalar=ostd_t[:, 1, 1:2], in1=go_s[:, 1, :],
                                       op0=ALU.mult, op1=ALU.add).then_inc(last_chain, 1)
                dve.wait_ge(last_chain, 4 * j + 3 + ONE)
                V.tensor_tensor(y, y, h1_t[:, 1, :], ALU.add).then_inc(last_chain, 1)

            def ring_item(s, item, m, parity):
                dve.wait_ge(a_ready, m + 1)
                V.tensor_reduce(half_max[:, s % 2, item:item + 1], ps_a[:, parity, :], AX.X, ALU.max).then_inc(a_used, 1)

            def ring_row(g, s, m, parity):
                dve.wait_ge(a_ready, m + 1)
                need(dve, row_in[s % 2], 64 * g + 32 * (s // 2))
                V.tensor_copy(max_rows[:, s % 2, :], ps_a[0:16, parity, 0:128]).then_inc(max_chain, 1)
                dve.wait_ge(max_chain, 16 * g + 4 * s + 4)
                dve.sem_inc(a_used, 1)

            def max_negated(g, s, m_last):
                dve.wait_ge(a_used, m_last + 1)
                V.tensor_reduce(neg_max[:, s % 2, :], half_max[:, s % 2, :].rearrange("p (t h) -> p t h", h=2), AX.X, ALU.max,
                                negate=True).then_inc(max_chain, 1)

            def max_high(g, s):
                dve.wait_ge(max_chain, 16 * g + 4 * s + 1)
                V.tensor_copy(max_parts[:, s % 2, 0:8], neg_max[:, s % 2, :]).then_inc(max_chain, 1)

            def max_low(g, s):
                dve.wait_ge(max_chain, 16 * g + 4 * s + 2)
                V.tensor_tensor(max_parts[:, s % 2, 8:16], neg_max[:, s % 2, :], max_parts[:, s % 2, 0:8].bitcast(F32),
                                ALU.subtract).then_inc(max_chain, 1)

            def low(i, step):
                n, k = 32 * i + step, step % 8
                dve.wait_ge(exp_done, n + 1)
                need(dve, pv_done, n - 3)
                V.tensor_tensor(p_lo[:, k % 4, :], p32[:, k % 4, :], p_hi[:, k % 4, :], ALU.subtract).then_inc(low_dve, 1)

            def add_parts(g, s, half):
                v = 4 * g + s
                dve.wait_ge(pv_done, 8 * v + 4 * half + 4)
                V.tensor_reduce(o_sum[:], ps_o[:, :, 1:VP].rearrange("p t (c d) -> p t d c", c=3), AX.X, ALU.add
                                ).then_inc(o_chain, 1)
                V.reciprocal(o_rcp[:], ps_o[:, :, 0]).then_inc(o_chain, 1)

            def normalise(g, s, half):
                v = 4 * g + s
                dve.wait_ge(o_chain, 3 * (2 * v + half) + 2)
                need(dve, att_out[half], 16 * v)
                V.scalar_tensor_tensor(out=o_out[:, half, :, :], in0=o_sum[:], scalar=ATT_SCALE,
                                       in1=o_rcp[:].unsqueeze(2).to_broadcast([128, 4, HD]),
                                       op0=ALU.mult, op1=ALU.mult).then_inc(o_chain, 1)

            for a in range(2):
                take(0, a, lead=True)
            with dve.Fori(0, LEAD - 1) as p:
                for a in range(2):
                    tile_stats(p + 1, a)
                for fill in range(2, 8):
                    take(p, fill, lead=True)
                    if fill > 5:
                        v_high(p, fill - 6)
                for a in range(2):
                    take(p + 1, a, lead=True)
                for a in range(2):
                    v_middle(p, a)
            for step in range(LEAD_STEPS):
                for m in range(*LEAD_SPAN.get(step, (0, 0))):
                    v, item = lead_item(m)
                    if item == 16:
                        ring_row(0, v, m, m % 2)
                    else:
                        ring_item(v, item, m, m % 2)
                    if (v, item) == (0, 15):
                        max_negated(0, 0, m)
                        max_high(0, 0)
                        max_low(0, 0)
                fill = evacuated(LEAD_STAGE, step)
                if fill is not None:
                    take(LEAD - 1, fill, lead=True)
                    if fill > 5:
                        v_high(LEAD - 1, fill - 6)
                if step in (2, 5):
                    tile_stats(LEAD, step // 3)
            for a in range(2):
                v_middle(LEAD - 1, a)

            def iteration(i, tiles, norms, outs, first=False, last=False):
                pair = i - FIRST_OUTS
                for s in range(4):
                    for k in range(8):
                        step = 8 * s + k
                        uses = ring_uses(i, s, k, last)

                        def ring(some):
                            for g, sa, item, m, parity in some:
                                if item == 16:
                                    ring_row(g, sa, m, parity)
                                else:
                                    ring_item(sa, item, m, parity)

                        ended = {3: (i - (s == 0), (s - 1) % 4, 1), 7: (i, s, 0)}.get(k)
                        if first and (s, k) == (0, 3):
                            ended = None
                        split = None if last and s == 3 else (i + (s + 1) // 4, (s + 1) % 4)
                        if split and k == 4:
                            max_high(*split)
                        if ended:
                            add_parts(*ended)
                        if tiles and evacuated(PAIR_STAGE, step - 1) in (2, 3, 4, 5):
                            take(i + LEAD, evacuated(PAIR_STAGE, step - 1))
                        ring(uses[:1])
                        if ended:
                            normalise(*ended)
                        if split and k == 4:
                            max_low(*split)
                        if tiles and evacuated(PAIR_STAGE, step - 1) in (6, 7):
                            v_high(i + LEAD, evacuated(PAIR_STAGE, step - 1) - 6)
                        before = (step - 2) % 32
                        if before not in POOL_LOW | DVE_LOW_EARLY and not (first and step == 0):
                            low(i - (step < 2), before)
                        ring(uses[1:])
                        if split and k == 3:
                            max_negated(*split, A_LEAD + 17 * (4 * i + s) + 7)
                        if step - 1 in DVE_LOW_EARLY:
                            low(i, step - 1)
                        fill = evacuated(PAIR_STAGE, step)
                        if tiles and fill in (0, 1, 6, 7):
                            take(i + LEAD, fill)
                        if outs and step - 1 in OUT_STAGE:
                            a, part = OUT_STAGE[step - 1]
                            if part == 0:
                                out_low(2 * pair + a, a)
                            if part == 2:
                                out_sum(pair, a)
                        if norms and step in LN_STEP:
                            tile_stats(i + LEAD + 1, LN_STEP[step])
                        if tiles and step in V_MIDDLE_STEP:
                            v_middle(i + LEAD, V_MIDDLE_STEP[step])
                        if outs and step in OUT_STATS_STEP:
                            a = OUT_STATS_STEP[step]
                            out_stats(2 * pair + a, a)

            iteration(0, True, True, False, first=True)
            with dve.Fori(1, FIRST_OUTS) as i:
                iteration(i, True, True, False)
            with dve.Fori(FIRST_OUTS, LAST_TILES - 1) as i:
                iteration(i, True, True, True)
            iteration(LAST_TILES - 1, True, False, True)
            with dve.Fori(LAST_TILES, ITERS - 1) as i:
                iteration(i, False, False, True)
            iteration(ITERS - 1, False, False, True, last=True)
            low(ITERS - 1, 30)
            add_parts(ITERS - 1, 3, 1)
            normalise(ITERS - 1, 3, 1)
            for a in range(2):
                out_low(2 * END + a, a, end=True)
            with dve.Fori(END, ITERS - 1) as m:
                for a in range(2):
                    end_sum(m, a)
                    out_stats(2 * m + a, a)
                for a in range(2):
                    out_low(2 * m + 2 + a, a, end=True)
                last_norm(m)
            for a in range(2):
                end_sum(ITERS - 1, a)
                out_stats(2 * (ITERS - 1) + a, a)
            last_norm(ITERS - 1)

        @block.gpsimd
        def _(pool):
            G = nc.gpsimd
            for semaphore in start_at_one:
                pool.sem_inc(semaphore, ONE)
            pool.sem_inc(tile_ev, PAIR_BEFORE)
            G.memset(minus_half[:], -0.5)
            G.memset(eps_s[:], EPS)
            G.memset(zero_s[:], 0.0)
            G.memset(ident[:], 0.0).then_inc(id_zero, 1)
            pool.wait_ge(id_zero, 1)
            G.affine_select(out=ident[:], in_=ident[:], compare_op=ALU.not_equal, fill=1.0, base=0,
                            pattern=[[-1, 128]], channel_multiplier=1).then_inc(id_ready, 1)
            pool.wait_ge(id_ready, 1)
            for a in range(2):
                G.dma_start(mark_d[a], ident[0:1, 0:16]).then_inc(y_out[a], 16)

            def power(mv, std, chain):
                G.tensor_tensor(std[:, 1:2], mv[:, 1:2], eps_s[:], ALU.add)
                G.tensor_tensor(std[:, 0:1], zero_s[:], mv[:, 0:1], ALU.subtract)
                pool.drain()
                G.tensor_tensor(std[:, 1:2], std[:, 1:2], minus_half[:], ALU.pow).then_inc(chain, 1)
                pool.drain()

            def norm_scale(pair, a):
                pool.wait_ge(ln_stat, 2 * pair + a + 1)
                need(pool, tile_mm, 8 * (pair - 1) + a + 1)
                power(mv_t[:, a, :], std_t[:, a, :], ln_pool)
                G.tensor_scalar(h_tile[:, a, :], x_tile[:, a, :], std_t[:, a, 0:1], std_t[:, a, 1:2], ALU.add, ALU.mult
                                ).then_inc(ln_pool, 1)

            def norm_gain(pair, a):
                h = h_tile[:, a, :]
                pool.wait_ge(ln_pool, 8 * pair + 4 * a + 2)
                pool.wait_ge(gq_in, 16 * pair + 16)
                G.tensor_tensor(h, h, gq_s[:, 0, :], ALU.mult).then_inc(ln_pool, 1)
                pool.wait_ge(ln_pool, 8 * pair + 4 * a + 3)
                G.tensor_tensor(h, h, gq_s[:, 1, :], ALU.add).then_inc(ln_pool, 1)

            def v_take_high(pair, a):
                pool.wait_ge(v_dve, 4 * pair + 1 + a)
                rest = v_rest[:, a, :].rearrange("p (h d) -> p h d", h=H)
                G.tensor_tensor(rest, rest, v_parts[:, a, :, 1:1 + HD], ALU.subtract).then_inc(v_pool, 1)

            def v_take_middle(pair, a):
                pool.wait_ge(v_dve, 4 * pair + 3 + a)
                rest = v_rest[:, a, :].rearrange("p (h d) -> p h d", h=H)
                G.tensor_tensor(v_parts[:, a, :, 1 + 2 * HD:VP], rest, v_parts[:, a, :, 1 + HD:1 + 2 * HD], ALU.subtract
                                ).then_inc(v_pool, 1)

            def residual(pair, a):
                pool.wait_ge(res_in[a], 16 * pair + 16)
                G.tensor_tensor(res_t[:, a, :], res_t[:, a, :], bp_s[:], ALU.add).then_inc(res_ready, 1)

            def out_scale(pair, a, count, gains=None):
                pool.wait_ge(out_stat, 2 * pair + a + 1)
                pool.wait_ge(y_out[a], 16 * pair + 16)
                power(omv_t[:, a, :], ostd_t[:, a, :], out_pool)
                y = y_t[:, a, :]
                G.tensor_scalar(y, h1_t[:, a, :], ostd_t[:, a, 0:1], ostd_t[:, a, 1:2], ALU.add, ALU.mult
                                ).then_inc(out_pool, 1)
                pool.wait_ge(out_pool, count + 2)
                pool.wait_ge(go_in, 16 * pair + 16 if gains is None else gains)
                G.tensor_tensor(y, y, go_s[:, 0, :], ALU.mult).then_inc(out_pool, 1)

            def out_finish(pair, a, count):
                y = y_t[:, a, :]
                pool.wait_ge(out_pool, count + 3)
                G.tensor_tensor(y, y, go_s[:, 1, :], ALU.add).then_inc(out_pool, 1)
                pool.wait_ge(out_pool, count + 4)
                G.tensor_tensor(y, y, h1_t[:, a, :], ALU.add).then_inc(out_pool, 1)
                pool.wait_ge(out_pool, count + 5)
                G.dma_start(out_rows[bass.ds((2 * pair + a) * 128, 128), :], y).then_inc(y_out[a], 16)

            def end_pair(m):
                count = 5 * (m + END) + ONE
                out_scale(m, 0, count, gains=16 * END + 16)
                pool.wait_ge(out_stat, 2 * m + 2)
                pool.wait_ge(last_chain, 4 * (m - END) + ONE)
                power(omv_t[:, 1, :], ostd_t[:, 1, :], last_std)
                out_finish(m, 0, count)

            def low(i, step):
                n, k = 32 * i + step, step % 8
                pool.wait_ge(exp_done, n + 1)
                need(pool, pv_done, n - 3)
                G.tensor_tensor(p_lo[:, k % 4, :], p32[:, k % 4, :], p_hi[:, k % 4, :], ALU.subtract).then_inc(low_pool, 1)

            def norm(pair, a):
                norm_scale(pair, a)
                norm_gain(pair, a)

            def v_rests(pair):
                for a in range(2):
                    v_take_high(pair, a)
                for a in range(2):
                    v_take_middle(pair, a)

            pool.wait_ge(bv_ready, 2)
            for a in range(2):
                norm(0, a)
            with pool.Fori(0, LEAD - 1) as p:
                for a in range(2):
                    norm(p + 1, a)
                v_rests(p)
            for a in range(2):
                norm(LEAD, a)
            v_rests(LEAD - 1)

            def iteration(i, tiles, norms, outs):
                pair = i - FIRST_OUTS
                ahead = i + LEAD
                for step in range(32):
                    if step in POOL_LOW:
                        low(i, step)
                    if norms and step in NORM_SCALE_STEP:
                        norm_scale(ahead + 1, NORM_SCALE_STEP[step])
                    if norms and step in NORM_GAIN_STEP:
                        norm_gain(ahead + 1, NORM_GAIN_STEP[step])
                    if tiles and step in V_HIGH_STEP:
                        v_take_high(ahead, V_HIGH_STEP[step])
                    if tiles and step in V_LOW_STEP:
                        v_take_middle(ahead, V_LOW_STEP[step])
                    if outs and step in RESIDUAL_STEP:
                        residual(pair, RESIDUAL_STEP[step])
                    if outs and step in OUT_SCALE_STEP:
                        a = OUT_SCALE_STEP[step]
                        out_scale(pair, a, 10 * pair + 5 * a + ONE)
                    if outs and step in OUT_FINISH_STEP:
                        a = OUT_FINISH_STEP[step]
                        out_finish(pair, a, 10 * pair + 5 * a + ONE)

            iteration(0, True, True, False)
            with pool.Fori(1, FIRST_OUTS) as i:
                iteration(i, True, True, False)
            with pool.Fori(FIRST_OUTS, LAST_TILES - 1) as i:
                iteration(i, True, True, True)
            iteration(LAST_TILES - 1, True, False, True)
            with pool.Fori(LAST_TILES, ITERS - 1) as i:
                iteration(i, False, False, True)
            iteration(ITERS - 1, False, False, True)
            residual(END, 0)
            with pool.Fori(END, ITERS - 1) as m:
                end_pair(m)
                residual(m + 1, 0)
            end_pair(ITERS - 1)


NAMES = ["x", "cond_1024"] + ["L0_cond_" + n for n in (
    "ln_g", "ln_b", "Wg", "bg", "Wb", "bb", "Wqkv", "bqkv", "Wp", "bp")]


def kernel(**inputs):
    import numpy as np
    import concourse.bacc as bacc
    from concourse.bass_utils import run_bass_kernel_spmd

    nc = bacc.Bacc("TRN2", target_bir_lowering=False, num_devices=1)
    arrays, args = {}, []
    for name in NAMES:
        a = np.ascontiguousarray(inputs[name])
        arrays[f"in_{name}"] = a
        args.append(nc.dram_tensor(f"in_{name}", a.shape, mybir.dt.from_np(a.dtype), kind="ExternalInput").ap())
    out = nc.dram_tensor("out_y", inputs["x"].shape, F32, kind="ExternalOutput").ap()
    conditioned_attention(nc, *args, out)
    result = run_bass_kernel_spmd(nc, [arrays], core_ids=[0])
    return result.results[0]["out_y"]
```
